# Optimizing a Trainium2 kernel written in Bass

```python
import numpy as np
import jax
import jax.numpy as jnp

def _softmax(x, axis=-1):
    return jax.nn.softmax(x, axis=axis)

def _gelu(x):
    return jax.nn.gelu(x, approximate=True)

def _silu(x):
    return jax.nn.silu(x)

def _sigmoid(x):
    return jax.nn.sigmoid(x)

def _layernorm(x, axis=-1, eps=1e-05):
    m = jnp.mean(x, axis=axis, keepdims=True)
    v = jnp.var(x, axis=axis, keepdims=True)
    return (x - m) / jnp.sqrt(v + eps)

def _scatter_add(tgt, idx, src, axis=0):
    return tgt.at[idx].add(src)

def _segment_sum(src, seg, n):
    return jax.ops.segment_sum(src, seg, n)
kernel_name = 'mk_hybrid_d1_jaxref_r8_e00b52'

def setup_inputs(seed: int=0):
    np.random.seed(seed)
    _w = jnp.asarray

    def _L0_attn_a_setup():
        import jax, jax.numpy as jnp
        import numpy as np
        DIM = 128
        HEADS = 16
        DIM_HEAD = 64
        NUM_FREQS = 16
        INNER = HEADS * DIM_HEAD

        def rotate_half(x):
            x1 = x[..., ::2]
            x2 = x[..., 1::2]
            return jnp.concatenate((-x2, x1), axis=-1)

        def rope_fourier_cache(seq_len, head_dim, num_freqs):
            freqs = 10000.0 ** (-jnp.arange(0, head_dim, 2, dtype=jnp.float32) / head_dim)
            pos = jnp.arange(seq_len, dtype=jnp.float32)[:, None]
            angles = pos * freqs
            sin = jnp.sin(angles)
            cos = jnp.cos(angles)
            sin = jnp.stack([sin, sin], axis=-1).reshape(seq_len, head_dim)
            cos = jnp.stack([cos, cos], axis=-1).reshape(seq_len, head_dim)
            ffreqs = jnp.arange(1, num_freqs + 1, dtype=jnp.float32)
            p = jnp.arange(seq_len, dtype=jnp.float32)[:, None]
            fourier = jnp.concatenate([jnp.sin(p * ffreqs), jnp.cos(p * ffreqs)], axis=-1)
            return (sin, cos, fourier)
        key = jax.random.key(seed)
        ks = jax.random.split(key, 6)
        b, n = (4, 256)
        x = jax.random.normal(ks[0], (b, n, DIM), dtype=jnp.float32)
        w_qkv = jax.random.normal(ks[1], (3 * INNER, DIM), dtype=jnp.float32) * DIM ** (-0.5)
        w_fproj = jax.random.normal(ks[2], (DIM_HEAD, 2 * NUM_FREQS), dtype=jnp.float32) * (2 * NUM_FREQS) ** (-0.5)
        b_fproj = jax.random.normal(ks[3], (DIM_HEAD,), dtype=jnp.float32) * 0.02
        w_out = jax.random.normal(ks[4], (DIM, INNER), dtype=jnp.float32) * INNER ** (-0.5)
        b_out = jax.random.normal(ks[5], (DIM,), dtype=jnp.float32) * 0.02
        return {'x': x, 'w_qkv': w_qkv, 'w_fproj': w_fproj, 'b_fproj': b_fproj, 'w_out': w_out, 'b_out': b_out}
    _L0_attn_a_in = _L0_attn_a_setup()

    def _L0_attn_b_setup():
        import jax, jax.numpy as jnp
        import numpy as np
        EMBED_DIM = 128
        NUM_HEADS = 16
        CHUNK_SIZE = 128
        BATCH = 4
        SEQ_LEN = 1024

        def _chunked_attention(x, wq, bq, wk, bk, wv, bv, wo, bo):
            B, S, E = x.shape
            H, T = (NUM_HEADS, CHUNK_SIZE)
            D = E // H
            C = S // T
            scale = 1.0 / float(np.sqrt(D))

            def proj(w, b):
                y = jnp.einsum('bse,fe->bsf', x, w) + b
                return y.reshape(B, C, T, H, D).transpose(0, 3, 1, 2, 4)
            q = proj(wq, bq)
            k = proj(wk, bk)
            v = proj(wv, bv)
            s_intra = jnp.einsum('bhctd,bhcsd->bhcts', q, k) * scale
            a_intra = jax.nn.softmax(s_intra, axis=-1)
            intra = jnp.einsum('bhcts,bhcsd->bhctd', a_intra, v)
            k_means = k.mean(axis=3)
            v_means = v.mean(axis=3)
            s_inter = jnp.einsum('bhctd,bhjd->bhctj', q, k_means) * scale
            chunk_pos = jnp.arange(C)
            causal = chunk_pos[:, None] >= chunk_pos[None, :]
            s_inter = jnp.where(causal[None, None, :, None, :], s_inter, -jnp.inf)
            a_inter = jax.nn.softmax(s_inter, axis=-1)
            inter = jnp.einsum('bhctj,bhjd->bhctd', a_inter, v_means)
            out = intra + inter
            out = out.transpose(0, 2, 3, 1, 4).reshape(B, S, E)
            return jnp.einsum('bse,fe->bsf', out, wo) + bo
        key = jax.random.key(seed)
        ks = jax.random.split(key, 9)
        E = EMBED_DIM
        s = 1.0 / np.sqrt(E)
        inp = {'hidden_states': jax.random.normal(ks[0], (BATCH, SEQ_LEN, E), dtype=jnp.float32), 'wq': jax.random.normal(ks[1], (E, E), dtype=jnp.float32) * s, 'bq': jax.random.normal(ks[2], (E,), dtype=jnp.float32) * s, 'wk': jax.random.normal(ks[3], (E, E), dtype=jnp.float32) * s, 'bk': jax.random.normal(ks[4], (E,), dtype=jnp.float32) * s, 'wv': jax.random.normal(ks[5], (E, E), dtype=jnp.float32) * s, 'bv': jax.random.normal(ks[6], (E,), dtype=jnp.float32) * s, 'wo': jax.random.normal(ks[7], (E, E), dtype=jnp.float32) * s, 'bo': jax.random.normal(ks[8], (E,), dtype=jnp.float32) * s}
        return inp
    _L0_attn_b_in = _L0_attn_b_setup()

    def _L0_ffn_setup():
        import jax, jax.numpy as jnp
        import numpy as np

        def _binarize(w):
            alpha = jax.lax.stop_gradient(jnp.mean(jnp.abs(w), axis=1, keepdims=True))
            bw = alpha * jnp.sign(w)
            return w + jax.lax.stop_gradient(bw - w)
        key = jax.random.key(seed)
        k1, k2, k3, k4, k5 = jax.random.split(key, 5)
        D, H = (128, 512)
        x = jax.random.normal(k1, (64, 196, D), dtype=jnp.float32)
        w1 = jax.random.normal(k2, (H, D), dtype=jnp.float32) * 0.02
        b1 = jax.random.normal(k3, (H,), dtype=jnp.float32) * 0.02
        w2 = jax.random.normal(k4, (D, H), dtype=jnp.float32) * 0.02
        b2 = jax.random.normal(k5, (D,), dtype=jnp.float32) * 0.02
        return {'x': x, 'w1': w1, 'b1': b1, 'w2': w2, 'b2': b2}
    _L0_ffn_in = _L0_ffn_setup()
    _d = {'L0_attn_a_x': _L0_attn_a_in['x'], 'L0_attn_a_w_qkv': _L0_attn_a_in['w_qkv'], 'L0_attn_a_w_fproj': _L0_attn_a_in['w_fproj'], 'L0_attn_a_b_fproj': _L0_attn_a_in['b_fproj'], 'L0_attn_a_w_out': _L0_attn_a_in['w_out'], 'L0_attn_a_b_out': _L0_attn_a_in['b_out'], 'L0_attn_b_wq': _L0_attn_b_in['wq'], 'L0_attn_b_bq': _L0_attn_b_in['bq'], 'L0_attn_b_wk': _L0_attn_b_in['wk'], 'L0_attn_b_bk': _L0_attn_b_in['bk'], 'L0_attn_b_wv': _L0_attn_b_in['wv'], 'L0_attn_b_bv': _L0_attn_b_in['bv'], 'L0_attn_b_wo': _L0_attn_b_in['wo'], 'L0_attn_b_bo': _L0_attn_b_in['bo'], 'L0_ffn_w1': _L0_ffn_in['w1'], 'L0_ffn_b1': _L0_ffn_in['b1'], 'L0_ffn_w2': _L0_ffn_in['w2'], 'L0_ffn_b2': _L0_ffn_in['b2']}
    _x0 = _d['L0_attn_a_x']
    _d['L0_attn_a_x'] = jax.random.normal(jax.random.fold_in(jax.random.key(seed), 1), (8, 512, 128), dtype=_x0.dtype)
    del _x0
    return _d

def reference(L0_attn_a_x, L0_attn_a_w_qkv, L0_attn_a_w_fproj, L0_attn_a_b_fproj, L0_attn_a_w_out, L0_attn_a_b_out, L0_attn_b_wq, L0_attn_b_bq, L0_attn_b_wk, L0_attn_b_bk, L0_attn_b_wv, L0_attn_b_bv, L0_attn_b_wo, L0_attn_b_bo, L0_ffn_w1, L0_ffn_b1, L0_ffn_w2, L0_ffn_b2):

    def _L0_attn_a_ref(x, w_qkv, w_fproj, b_fproj, w_out, b_out):
        import jax, jax.numpy as jnp
        import numpy as np
        DIM = 128
        HEADS = 16
        DIM_HEAD = 64
        NUM_FREQS = 16
        INNER = HEADS * DIM_HEAD

        def rotate_half(x):
            x1 = x[..., ::2]
            x2 = x[..., 1::2]
            return jnp.concatenate((-x2, x1), axis=-1)

        def rope_fourier_cache(seq_len, head_dim, num_freqs):
            freqs = 10000.0 ** (-jnp.arange(0, head_dim, 2, dtype=jnp.float32) / head_dim)
            pos = jnp.arange(seq_len, dtype=jnp.float32)[:, None]
            angles = pos * freqs
            sin = jnp.sin(angles)
            cos = jnp.cos(angles)
            sin = jnp.stack([sin, sin], axis=-1).reshape(seq_len, head_dim)
            cos = jnp.stack([cos, cos], axis=-1).reshape(seq_len, head_dim)
            ffreqs = jnp.arange(1, num_freqs + 1, dtype=jnp.float32)
            p = jnp.arange(seq_len, dtype=jnp.float32)[:, None]
            fourier = jnp.concatenate([jnp.sin(p * ffreqs), jnp.cos(p * ffreqs)], axis=-1)
            return (sin, cos, fourier)
        b, n, _ = x.shape
        scale = DIM_HEAD ** (-0.5)
        qkv = x @ w_qkv.T
        q, k, v = jnp.split(qkv, 3, axis=-1)

        def to_heads(t):
            return t.reshape(b, n, HEADS, DIM_HEAD).transpose(0, 2, 1, 3)
        q, k, v = (to_heads(q), to_heads(k), to_heads(v))
        sin, cos, fourier = rope_fourier_cache(n, DIM_HEAD, NUM_FREQS)
        fenc = fourier @ w_fproj.T + b_fproj
        fenc = fenc[None, None]
        q = q * cos + rotate_half(q) * sin + fenc
        k = k * cos + rotate_half(k) * sin + fenc
        dots = jnp.einsum('bhid,bhjd->bhij', q, k) * scale
        attn = jax.nn.softmax(dots, axis=-1)
        out = jnp.einsum('bhij,bhjd->bhid', attn, v)
        out = out.transpose(0, 2, 1, 3).reshape(b, n, INNER)
        return out @ w_out.T + b_out

    def _L0_attn_b_ref(hidden_states, wq, bq, wk, bk, wv, bv, wo, bo):
        import jax, jax.numpy as jnp
        import numpy as np
        EMBED_DIM = 128
        NUM_HEADS = 16
        CHUNK_SIZE = 128
        BATCH = 4
        SEQ_LEN = 1024

        def _chunked_attention(x, wq, bq, wk, bk, wv, bv, wo, bo):
            B, S, E = x.shape
            H, T = (NUM_HEADS, CHUNK_SIZE)
            D = E // H
            C = S // T
            scale = 1.0 / float(np.sqrt(D))

            def proj(w, b):
                y = jnp.einsum('bse,fe->bsf', x, w) + b
                return y.reshape(B, C, T, H, D).transpose(0, 3, 1, 2, 4)
            q = proj(wq, bq)
            k = proj(wk, bk)
            v = proj(wv, bv)
            s_intra = jnp.einsum('bhctd,bhcsd->bhcts', q, k) * scale
            a_intra = jax.nn.softmax(s_intra, axis=-1)
            intra = jnp.einsum('bhcts,bhcsd->bhctd', a_intra, v)
            k_means = k.mean(axis=3)
            v_means = v.mean(axis=3)
            s_inter = jnp.einsum('bhctd,bhjd->bhctj', q, k_means) * scale
            chunk_pos = jnp.arange(C)
            causal = chunk_pos[:, None] >= chunk_pos[None, :]
            s_inter = jnp.where(causal[None, None, :, None, :], s_inter, -jnp.inf)
            a_inter = jax.nn.softmax(s_inter, axis=-1)
            inter = jnp.einsum('bhctj,bhjd->bhctd', a_inter, v_means)
            out = intra + inter
            out = out.transpose(0, 2, 3, 1, 4).reshape(B, S, E)
            return jnp.einsum('bse,fe->bsf', out, wo) + bo
        return _chunked_attention(hidden_states, wq, bq, wk, bk, wv, bv, wo, bo)

    def _L0_ffn_ref(x, w1, b1, w2, b2):
        import jax, jax.numpy as jnp
        import numpy as np

        def _binarize(w):
            alpha = jax.lax.stop_gradient(jnp.mean(jnp.abs(w), axis=1, keepdims=True))
            bw = alpha * jnp.sign(w)
            return w + jax.lax.stop_gradient(bw - w)
        bw1 = _binarize(w1)
        h = jnp.einsum('bsd,hd->bsh', x, bw1) + b1
        h = jax.nn.gelu(h, approximate=False)
        bw2 = _binarize(w2)
        out = jnp.einsum('bsh,dh->bsd', h, bw2) + b2
        return out
    x = L0_attn_a_x
    x = x + _L0_attn_a_ref(_layernorm(x, axis=-1), L0_attn_a_w_qkv, L0_attn_a_w_fproj, L0_attn_a_b_fproj, L0_attn_a_w_out, L0_attn_a_b_out)
    x = x + _L0_ffn_ref(_layernorm(x, axis=-1), L0_ffn_w1, L0_ffn_b1, L0_ffn_w2, L0_ffn_b2)
    x = x + _L0_attn_b_ref(_layernorm(x, axis=-1), L0_attn_b_wq, L0_attn_b_bq, L0_attn_b_wk, L0_attn_b_bk, L0_attn_b_wv, L0_attn_b_bv, L0_attn_b_wo, L0_attn_b_bo)
    x = x + _L0_ffn_ref(_layernorm(x, axis=-1), L0_ffn_w1, L0_ffn_b1, L0_ffn_w2, L0_ffn_b2)
    return x

_drawn_inputs = setup_inputs


def setup_inputs(seed=0):
    import zlib

    import numpy as np

    out = dict(_drawn_inputs(seed))
    spreads = {}
    factors = {'L0_attn_a_b_fproj': 8.0, 'L0_attn_b_bq': 4.338, 'L0_attn_b_bk': 8.0, 'L0_ffn_b1': 6.143}
    for name, (base, spread) in spreads.items():
        noise = np.random.default_rng([zlib.crc32(name.encode()), seed]).standard_normal(out[name].shape)
        drawn = base * np.exp(spread * noise) if base else spread * noise
        out[name] = jnp.asarray(drawn.astype(out[name].dtype))
    for name, factor in factors.items():
        out[name] = (out[name] * factor).astype(out[name].dtype)
    return out
```

```python
from contextlib import ExitStack

import numpy as np

import concourse.bass as bass
from concourse import mybir

F32 = mybir.dt.float32
F16 = mybir.dt.float16
ALU = mybir.AluOpType
ACT = mybir.ActivationFunctionType
AX = mybir.AxisListType

P = 128
BATCH, SEQ, DIM = 8, 512, 128
TOKENS = BATCH * SEQ
TILES = TOKENS // P
BLOCK = 512
TPB = BLOCK // P
BLOCKS = TOKENS // BLOCK
EPS = 1e-5
WSCALE = 64.0

A_HEADS, A_HEAD = 16, 64
A_INNER = A_HEADS * A_HEAD
A_PAIRS = A_HEADS // 2
A_SCALE = float(A_HEAD) ** -0.5
FREQS = 16
Q, QR, K, KR, V = range(5)

B_HEADS, B_HEAD, CHUNK = 16, 8, 128
CHUNKS = SEQ // CHUNK
B_GROUPS = B_HEADS // 4
B_SCALE = float(B_HEAD) ** -0.5

HIDDEN = 512
HT = HIDDEN // P


def at_least(eng, sem, value):
    if not isinstance(value, int) or value > 0:
        eng.wait_ge(sem, value)


class Space:

    def __init__(self, nc, ctx, tag):
        self.nc, self.ctx, self.tag = nc, ctx, tag

    def sb(self, name, shape, dt):
        return self.ctx.enter_context(self.nc.sbuf_tensor(f"{self.tag}_{name}", shape, dt))

    def ps(self, name, shape):
        return self.ctx.enter_context(self.nc.psum_tensor(f"{self.tag}_{name}", shape, F32))

    def sem(self, name):
        return self.ctx.enter_context(self.nc.semaphore(f"{self.tag}_{name}"))


class Norm:

    def __init__(self, s, ident, minus_half, bank):
        self.ident, self.minus_half, self.bank = ident, minus_half, bank
        self.stats = s.sb("stats", [P, TPB, 6], F32)
        self.mean = s.sb("mean", [P, TPB], F32)
        self.apart = s.sb("apart", [P, TPB], F32)
        self.squares = s.sb("squares", [P, TPB], F32)
        self.var_eps = s.sb("var_eps", [P, TPB], F32)
        self.rstd = s.sb("rstd", [P, TPB], F32)
        self.normed = s.sb("normed", [P, TPB, DIM], F32)
        self.stats_ready = s.sem("stats_ready")
        self.moments_ready = s.sem("moments_ready")
        self.moment_steps = s.sem("moment_steps")
        self.rstd_ready = s.sem("rstd_ready")
        self.normed_ready = s.sem("normed_ready")
        self.turned = s.sem("turned")
        self.hi_ready = s.sem("xt_hi_ready")
        self.xt_ready = s.sem("xt_ready")

    def dve_moments(self, dve, n, x4):
        half, st = DIM // 2, self.stats
        for t in range(TPB):
            dve.bn_stats(st[:, t, :], x4[:, t, :]).then_inc(self.stats_ready, 1)
        dve.wait_ge(self.stats_ready, TPB * n + TPB)
        dve.tensor_tensor(self.mean[:], st[:, :, 1], st[:, :, 4], ALU.add).then_inc(self.moment_steps, 1)
        dve.tensor_tensor(self.apart[:], st[:, :, 1], st[:, :, 4], ALU.subtract).then_inc(self.moment_steps, 1)
        dve.tensor_tensor(self.squares[:], st[:, :, 2], st[:, :, 5], ALU.add).then_inc(self.moment_steps, 1)
        dve.wait_ge(self.moment_steps, 6 * n + 3)
        dve.tensor_scalar(self.mean[:], self.mean[:], 0.5, None, ALU.mult).then_inc(self.moment_steps, 1)
        dve.scalar_tensor_tensor(out=self.apart[:], in0=self.apart[:], scalar=half / 2.0, in1=self.apart[:],
                                 op0=ALU.mult, op1=ALU.mult).then_inc(self.moment_steps, 1)
        dve.wait_ge(self.moment_steps, 6 * n + 5)
        dve.tensor_tensor(self.squares[:], self.squares[:], self.apart[:], ALU.add).then_inc(self.moment_steps, 1)
        dve.wait_ge(self.moment_steps, 6 * n + 6)
        dve.tensor_scalar(self.var_eps[:], self.squares[:], 1.0 / DIM, EPS, ALU.mult,
                          ALU.add).then_inc(self.moments_ready, 1)

    def pool_rstd(self, pool, n):
        pool.wait_ge(self.moments_ready, n + 1)
        pool.tensor_tensor(self.rstd[:], self.var_eps[:], self.minus_half[:, 0:TPB], ALU.pow).then_inc(self.rstd_ready, 1)

    def dve_apply(self, dve, n, x4):
        dve.wait_ge(self.rstd_ready, n + 1)
        for t in range(TPB):
            dve.tensor_scalar(self.normed[:, t, :], x4[:, t, :], self.mean[:, t:t + 1], self.rstd[:, t:t + 1],
                              ALU.subtract, ALU.mult).then_inc(self.normed_ready, 1)

    def pe_turn(self, pe, n):
        pe.wait_ge(self.normed_ready, TPB * n + TPB)
        for t in range(TPB):
            last = pe.transpose(self.bank[:, t * P:(t + 1) * P], self.normed[:, t, :], self.ident[:])
        last.then_inc(self.turned, 1)

    def act_hi(self, act, n, hi):
        act.wait_ge(self.turned, n + 1)
        act.activation(hi, self.bank[:], ACT.Copy).then_inc(self.hi_ready, 1)

    def dve_lo(self, dve, n, hi, lo):
        dve.wait_ge(self.hi_ready, n + 1)
        dve.tensor_tensor(lo, self.bank[:], hi, ALU.subtract).then_inc(self.xt_ready, 1)


def three_products(pe, out, stat_hi, stat_lo, mov_hi, mov_lo, first=True, last=True):
    pe.matmul(out, stat_hi, mov_hi, start=first, stop=False)
    pe.matmul(out, stat_hi, mov_lo, start=False, stop=False)
    return pe.matmul(out, stat_lo, mov_hi, start=False, stop=last)


def attention_a(nc, d, x_all, ident, minus_half):
    with ExitStack() as keep:
        s = Space(nc, keep, "a")
        xt_hi = s.sb("xt_hi", [P, TOKENS], F16)
        xt_lo = s.sb("xt_lo", [P, TOKENS], F16)
        w_hi = s.sb("w_hi", [P, 5, A_INNER], F16)
        w_lo = s.sb("w_lo", [P, 5, A_INNER], F16)
        wo_hi = s.sb("wo_hi", [P, A_PAIRS, DIM], F16)
        wo_lo = s.sb("wo_lo", [P, A_PAIRS, DIM], F16)
        cos = s.sb("cos", [P, 2, SEQ], F32)
        sin = s.sb("sin", [P, 2, SEQ], F32)
        four = s.sb("four", [P, 2, SEQ], F32)
        attention_a_prepare(nc, d, x_all, ident, minus_half, xt_hi, xt_lo, w_hi, w_lo, wo_hi, wo_lo, cos, sin, four)
        attention_a_heads(nc, x_all, ident, xt_hi, xt_lo, w_hi, w_lo, wo_hi, wo_lo, cos, sin, four)


def attention_a_prepare(nc, d, x_all, ident, minus_half, xt_hi, xt_lo, w_hi, w_lo, wo_hi, wo_lo, cos, sin, four):
    with ExitStack() as ctx:
        s = Space(nc, ctx, "ap")
        w_raw = s.sb("w_raw", [P, 5, A_INNER], F32)
        wo_raw = s.sb("wo_raw", [P, A_PAIRS, DIM], F32)
        fourier = s.sb("fourier", [2 * FREQS, SEQ], F32)
        w_four = s.sb("w_four", [2 * FREQS, P], F32)
        b_four = s.sb("b_four", [P, 1], F32)
        b_out = s.sb("b_out", [P, DIM], F32)
        turn_bank = s.ps("turn_bank", [P, BLOCK])
        four_bank = s.ps("four_bank", [P, SEQ])
        norm = Norm(s, ident, minus_half, turn_bank)
        x_in = s.sem("x_in")
        consts_in = s.sem("consts_in")
        weights_in = s.sem("weights_in")
        half_set = s.sem("half_set")
        weights_hi = s.sem("weights_hi")
        weights_ready = s.sem("weights_ready")
        four_mm = s.sem("four_mm")
        four_k_ready = s.sem("four_k_ready")
        four_ready = s.sem("four_ready")
        bias_added = s.sem("bias_added")
        block = ctx.enter_context(nc.Block())
        CONSTS = 9

        @block.sync
        def _(sp):
            sp.dma_start(ident[:], d["ident"]).then_inc(consts_in, 16)
            sp.dma_start(fourier[:], d["fourier"]).then_inc(consts_in, 16)
            sp.dma_start(w_four[:], d["w_four"]).then_inc(consts_in, 16)
            sp.dma_start(b_four[:], d["b_four"]).then_inc(consts_in, 16)
            sp.dma_start(b_out[:], d["b_out_a"]).then_inc(consts_in, 16)
            for half in range(2):
                sp.dma_start(cos[:, half, :], d["cos"][half]).then_inc(consts_in, 16)
                sp.dma_start(sin[:, half, :], d["sin"][half]).then_inc(consts_in, 16)
            sp.dma_start(w_raw[:], d["w_a"]).then_inc(weights_in, 16)
            sp.dma_start(wo_raw[:], d["wo_a"]).then_inc(weights_in, 16)

        @block.vector
        def _(dve):
            dve.memset(minus_half[:], -0.5).then_inc(half_set, 1)
            dve.wait_ge(x_in, 16)
            with dve.Fori(0, BLOCKS) as n:
                x4 = x_all[:, bass.ds(n * TPB, TPB), :]
                norm.dve_moments(dve, n, x4)
                norm.dve_apply(dve, n, x4)
                norm.dve_lo(dve, n, xt_hi[:, bass.ds(n * BLOCK, BLOCK)], xt_lo[:, bass.ds(n * BLOCK, BLOCK)])
            dve.wait_ge(four_k_ready, 1)
            dve.tensor_scalar(four[:, 0, :], four[:, 1, :], A_SCALE, None, ALU.mult).then_inc(four_ready, 1)
            for kind in range(5):
                dve.wait_ge(weights_hi, kind + 1)
                dve.scalar_tensor_tensor(out=w_lo[:, kind, :], in0=w_raw[:, kind, :], scalar=WSCALE,
                                         in1=w_hi[:, kind, :], op0=ALU.mult,
                                         op1=ALU.subtract).then_inc(weights_ready, 1)
            dve.wait_ge(weights_hi, 6)
            dve.scalar_tensor_tensor(out=wo_lo[:], in0=wo_raw[:], scalar=WSCALE, in1=wo_hi[:], op0=ALU.mult,
                                     op1=ALU.subtract).then_inc(weights_ready, 1)

        @block.gpsimd
        def _(pool):
            pool.wait_ge(half_set, 1)
            pool.wait_ge(consts_in, 16 * CONSTS)
            with pool.Fori(0, BLOCKS) as n:
                norm.pool_rstd(pool, n)
                pool.wait_ge(norm.normed_ready, TPB * n + TPB)
                for t in range(TPB):
                    x1 = x_all[:, bass.ds(n * TPB + t, 1), :].rearrange("p a c -> p (a c)")
                    pool.tensor_tensor(x1, x1, b_out[:], ALU.add).then_inc(bias_added, 1)

        @block.scalar
        def _(act):
            act.dma_start(x_all[:], d["x"]).then_inc(x_in, 16)
            act.wait_ge(weights_in, 32)
            for kind in range(5):
                act.activation(w_hi[:, kind, :], w_raw[:, kind, :], ACT.Copy, scale=WSCALE).then_inc(weights_hi, 1)
            act.activation(wo_hi[:], wo_raw[:], ACT.Copy, scale=WSCALE).then_inc(weights_hi, 1)
            with act.Fori(0, BLOCKS) as n:
                norm.act_hi(act, n, xt_hi[:, bass.ds(n * BLOCK, BLOCK)])
            act.wait_ge(four_mm, 1)
            act.activation(four[:, 1, :], four_bank[:], ACT.Identity, bias=b_four[:, 0:1]).then_inc(four_k_ready, 1)

        @block.tensor
        def _(pe):
            pe.wait_ge(consts_in, 16 * CONSTS)
            pe.matmul(four_bank[:], w_four[:], fourier[:], start=True, stop=True).then_inc(four_mm, 1)
            with pe.Fori(0, BLOCKS) as n:
                norm.pe_turn(pe, n)


def attention_a_heads(nc, x_all, ident, xt_hi, xt_lo, w_hi, w_lo, wo_hi, wo_lo, cos, sin, four):
    STEPS = BATCH * A_PAIRS
    HQ = 2
    HEADCOLS = A_HEAD + 1
    Q_COPIES, K_COPIES = 8, 4
    with ExitStack() as ctx:
        s = Space(nc, ctx, "ah")
        cos_part = s.sb("cos_part", [P, 2, SEQ], F32)
        sin_part = s.sb("sin_part", [P, 2, SEQ], F32)
        rot_hi = s.sb("rot_hi", [P, 2, SEQ], F16)
        rot_lo = s.sb("rot_lo", [P, 2, SEQ], F16)
        k_stack = s.sb("k_stack", [P, 2, 2, SEQ], F16)
        qh_stack = s.sb("qh_stack", [P, 2, 2, SEQ], F16)
        ql_stack = s.sb("ql_stack", [P, 2, 2, SEQ], F16)
        v_hi = s.sb("v_hi", [P, 2, TPB, 2, HEADCOLS], F16)
        v_lo = s.sb("v_lo", [P, 2, TPB, 2, A_HEAD], F16)
        neg_max = s.sb("neg_max", [P, 2, HQ], F32)
        probs = s.sb("probs", [P, 2, HQ, SEQ], F32)
        pt_hi = s.sb("pt_hi", [P, 2, TPB, HQ * P], F16)
        pt_lo = s.sb("pt_lo", [P, 2, TPB, HQ * P], F16)
        inv_sum = s.sb("inv_sum", [P, 2, HQ], F32)
        heads_out = s.sb("heads_out", [P, 2, TPB, P], F32)
        ot_hi = s.sb("ot_hi", [P, SEQ], F16)
        ot_lo = s.sb("ot_lo", [P, SEQ], F16)
        scores = s.ps("scores", [P, 2, HQ, SEQ])
        pt = s.ps("pt", [P, TPB, HQ * P])
        pv = s.ps("pv", [P, 4, P])
        side = s.ps("side", [P, SEQ])

        scores_ready = s.sem("scores_ready")
        max_ready = s.sem("max_ready")
        exp_ready = s.sem("exp_ready")
        pt_ready = s.sem("pt_ready")
        pt_hi_ready = s.sem("pt_hi_ready")
        pt_split = s.sem("pt_split")
        pv_ready = s.sem("pv_ready")
        inv_ready = s.sem("inv_ready")
        pv_taken = s.sem("pv_taken")
        side_ready = s.sem("side_ready")
        side_taken = s.sem("side_taken")
        fourier_added = [s.sem("fourier_added_q"), s.sem("fourier_added_k")]
        rotated = [s.sem("rotated_q"), s.sem("rotated_k")]
        rot_hi_ready = [s.sem("rot_hi_q"), s.sem("rot_hi_k")]
        rot_split = [s.sem("rot_split_q"), s.sem("rot_split_k")]
        stacked = [s.sem("stacked_q"), s.sem("stacked_k")]
        v_hi_ready = s.sem("v_hi_ready")
        v_split = s.sem("v_split")
        ot_hi_ready = s.sem("ot_hi_ready")
        ot_split = s.sem("ot_split")
        ones_set = s.sem("ones_set")

        LAST = STEPS - 1

        def side_count(g, slot):
            order = {"q": 0, "qr": 1, "k": 2, "kr": 3, "v": 4, "ot": 5, "op": 6}
            if not isinstance(g, int):
                return 7 * g + 7 + order[slot]
            if g == 0:
                return 9 + {"q": 0, "qr": 1, "k": 2, "kr": 3, "v": 4}[slot]
            if g < LAST - 1:
                return 7 * g + 7 + order[slot]
            base = 7 * (LAST - 1) + 7
            return base + {LAST - 1: {"v": 0, "ot": 1, "op": 2}, LAST: {"ot": 3, "op": 4},
                           STEPS: {"ot": 5, "op": 6}}[g][slot]

        def taken_count(g, slot):
            order = {"q": 0, "qr": 1, "k": 2, "kr": 3, "end": 4}
            if isinstance(g, int) and g == 0:
                return 8 + order[slot]
            if isinstance(g, int) and g >= LAST - 1:
                return 5 * (LAST - 1) + 7 + g - (LAST - 1)
            return 5 * g + 7 + order[slot]

        def run(eng, ahead, step, tail):
            ahead()
            step(0, 0)
            with eng.Fori(0, (STEPS - 4) // 2) as i:
                step(2 * i + 1, 1)
                step(2 * i + 2, 0)
            for g in range(STEPS - 3, STEPS):
                step(g, g % 2)
            tail()

        def is_last(g, steps=1):
            return isinstance(g, int) and g >= STEPS - steps

        def is_first(g):
            return isinstance(g, int) and g == 0

        def unit_after(g, u, ahead):
            return g + (u + ahead) // 4, (u + ahead) % 4

        block = ctx.enter_context(nc.Block())

        @block.sync
        def _(sp):
            def stack(n, par):
                for which in (0, 1):
                    sp.wait_ge(rot_split[which], n + 1)
                    if not isinstance(n, int) or n > 1:
                        sp.wait_ge(scores_ready, 4 * n - 4)
                    for h in range(2):
                        own = slice(h * A_HEAD, (h + 1) * A_HEAD)
                        for half in range(2):
                            to = slice(half * A_HEAD, (half + 1) * A_HEAD)
                            if which == 0:
                                sp.dma_start(qh_stack[to, par, h, :], rot_hi[own, 0, :]).then_inc(stacked[0], 16)
                                sp.dma_start(ql_stack[to, par, h, :], rot_lo[own, 0, :]).then_inc(stacked[0], 16)
                            else:
                                part = rot_lo if half else rot_hi
                                sp.dma_start(k_stack[to, par, h, :], part[own, 1, :]).then_inc(stacked[1], 16)

            def ahead():
                stack(0, 0)
                stack(1, 1)

            def step(g, par):
                if not is_last(g, 2):
                    stack(g + 2, par)

            run(sp, ahead, step, lambda: None)
            sp.wait_ge(stacked[0], 16 * Q_COPIES * STEPS)
            sp.wait_ge(stacked[1], 16 * K_COPIES * STEPS)

        @block.tensor
        def _(pe):
            def project(kind, n, count):
                at_least(pe, side_taken, count)
                w = bass.ds(n % A_PAIRS * P, P)
                x = bass.ds(n // A_PAIRS * SEQ, SEQ)
                three_products(pe, side[:], w_hi[:, kind, w], w_lo[:, kind, w], xt_hi[:, x],
                               xt_lo[:, x]).then_inc(side_ready, 1)

            def project_v(n):
                w = bass.ds(n % A_PAIRS * P, P)
                for t in range(TPB):
                    x = bass.ds(n // A_PAIRS * SEQ + t * P, P)
                    done = three_products(pe, side[:, t * P:(t + 1) * P], xt_hi[:, x], xt_lo[:, x],
                                          w_hi[:, V, w], w_lo[:, V, w])
                done.then_inc(side_ready, 1)

            def score(g, par, u):
                h, half = u // 2, u % 2
                if u == 0:
                    pe.wait_ge(stacked[0], 16 * Q_COPIES * (g + 1))
                    pe.wait_ge(stacked[1], 16 * K_COPIES * (g + 1))
                at_least(pe, exp_ready, HQ * (4 * g + u - 1))
                for t in range(HQ):
                    q = slice((half * HQ + t) * P, (half * HQ + t + 1) * P)
                    pe.matmul(scores[:, u % 2, t, :], qh_stack[:, par, h, q], k_stack[:, par, h, :],
                              start=True, stop=False)
                    done = pe.matmul(scores[:, u % 2, t, :], ql_stack[:, par, h, q], k_stack[:, par, h, :],
                                     start=False, stop=True)
                done.then_inc(scores_ready, 1)

            def turn(g, u):
                pe.wait_ge(exp_ready, HQ * (4 * g + u + 1))
                at_least(pe, pt_split, 4 * g + u)
                for j in range(TPB):
                    for t in range(HQ):
                        done = pe.transpose(pt[:, j, t * P:(t + 1) * P], probs[:, u % 2, t, j * P:(j + 1) * P],
                                            ident[:])
                done.then_inc(pt_ready, 1)

            def values(g, par, u):
                h = u // 2
                if u == 0:
                    pe.wait_ge(v_split, g + 1)
                pe.wait_ge(pt_split, 4 * g + u + 1)
                at_least(pe, pv_taken, 4 * g + u)
                for t in range(HQ):
                    for j in range(TPB):
                        p_hi = pt_hi[:, u % 2, j, t * P:(t + 1) * P]
                        p_lo = pt_lo[:, u % 2, j, t * P:(t + 1) * P]
                        pe.matmul(pv[:, t, 0:HEADCOLS], p_hi, v_hi[:, par, j, h, :], start=(j == 0), stop=False)
                        pe.matmul(pv[:, t, 0:A_HEAD], p_hi, v_lo[:, par, j, h, :], start=False, stop=False)
                        done = pe.matmul(pv[:, t, 0:HEADCOLS], p_lo, v_hi[:, par, j, h, :], start=False,
                                         stop=(j == TPB - 1))
                done.then_inc(pv_ready, 1)

            def turn_out(p, par):
                pe.wait_ge(pv_taken, 4 * p + 4)
                for t in range(TPB):
                    done = pe.transpose(side[:, t * P:(t + 1) * P], heads_out[:, par, t, :], ident[:])
                done.then_inc(side_ready, 1)

            def project_out(p):
                pe.wait_ge(ot_split, p + 1)
                pair = bass.ds(p % A_PAIRS, 1)
                o_hi = wo_hi[:, pair, :].rearrange("p a c -> p (a c)")
                o_lo = wo_lo[:, pair, :].rearrange("p a c -> p (a c)")
                for t in range(TPB):
                    tok = slice(t * P, (t + 1) * P)
                    done = three_products(pe, side[:, tok], ot_hi[:, tok], ot_lo[:, tok], o_hi, o_lo)
                done.then_inc(side_ready, 1)

            def after_score(g, par, u):
                g2, u2 = unit_after(g, u, 2)
                if not (is_last(g) and u >= 2):
                    score(g2, par if u < 2 else 1 - par, u2)

            def before_values(g, par, u):
                if u > 0:
                    values(g, par, u - 1)
                elif not is_first(g):
                    values(g - 1, 1 - par, 3)

            def step(g, par):
                for u, (cos_kind, sin_kind, cos_slot, sin_slot) in enumerate(((Q, QR, "q", "qr"), (K, KR, "k", "kr"))):
                    turn(g, u)
                    if not is_last(g, 2):
                        if is_first(g):
                            pe.wait_ge(v_split, 1)
                        elif u == 0:
                            pe.wait_ge(v_split, g + 1)
                        project(cos_kind, g + 2, taken_count(g, cos_slot))
                    after_score(g, par, u)
                    if not is_last(g, 2):
                        project(sin_kind, g + 2, taken_count(g, sin_slot))
                    before_values(g, par, u)
                turn(g, 2)
                if not is_last(g):
                    pe.wait_ge(side_taken, taken_count(g, "end"))
                    project_v(g + 1)
                after_score(g, par, 2)
                before_values(g, par, 2)
                if not is_first(g):
                    if is_last(g):
                        pe.wait_ge(side_taken, taken_count(g, "end"))
                    else:
                        pe.wait_ge(v_split, g + 2)
                    turn_out(g - 1, 1 - par)
                turn(g, 3)
                after_score(g, par, 3)
                if not is_first(g):
                    project_out(g - 1)
                before_values(g, par, 3)

            def ahead():
                for n in (0, 1):
                    for kind, name in ((Q, "q"), (QR, "qr"), (K, "k"), (KR, "kr")):
                        project(kind, n, 4 * n + kind)
                pe.wait_ge(side_taken, 8)
                project_v(0)
                score(0, 0, 0)
                score(0, 0, 1)

            def tail():
                values(LAST, LAST % 2, 3)
                pe.wait_ge(side_taken, taken_count(STEPS, "end"))
                turn_out(LAST, LAST % 2)
                project_out(LAST)

            run(pe, ahead, step, tail)

        @block.scalar
        def _(act):
            def exps(g, u):
                act.wait_ge(max_ready, 4 * g + u + 1)
                at_least(act, pt_ready, 4 * g + u - 1)
                for t in range(HQ):
                    act.activation(probs[:, u % 2, t, :], scores[:, u % 2, t, :], ACT.Exp,
                                   bias=neg_max[:, u % 2, t:t + 1]).then_inc(exp_ready, 1)

            def probs_hi(g, u):
                act.wait_ge(pt_ready, 4 * g + u + 1)
                at_least(act, pv_ready, 4 * g + u - 1)
                act.activation(pt_hi[:, u % 2, :, :], pt[:], ACT.Copy).then_inc(pt_hi_ready, 1)

            def rotated_hi(which, n):
                act.wait_ge(rotated[which], n + 1)
                at_least(act, stacked[which], 16 * (Q_COPIES, K_COPIES)[which] * n)
                act.activation(rot_hi[:, which, :], cos_part[:, which, :], ACT.Copy).then_inc(rot_hi_ready[which], 1)

            def value_hi(n, par, count):
                act.wait_ge(side_ready, count + 1)
                at_least(act, pv_ready, 4 * n - 4)
                act.activation(v_hi[:, par, :, :, 0:A_HEAD], side[:].rearrange("p (t h c) -> p t h c", t=TPB, h=2),
                               ACT.Copy, scale=1.0 / WSCALE).then_inc(v_hi_ready, 1)

            def out_hi(p, count):
                act.wait_ge(side_ready, count + 1)
                act.activation(ot_hi[:], side[:], ACT.Copy).then_inc(ot_hi_ready, 1)

            def next_exps(g, u):
                if not (is_last(g) and u == 3):
                    exps(*unit_after(g, u, 1))

            def step(g, par):
                for u in range(4):
                    if u == 3 and not is_first(g):
                        out_hi(g - 1, side_count(g, "ot"))
                    probs_hi(g, u)
                    if u == 2 and not is_last(g):
                        value_hi(g + 1, 1 - par, side_count(g, "v"))
                    next_exps(g, u)
                    if u >= 2 and not is_last(g, 2):
                        rotated_hi(u - 2, g + 2)

            def ahead():
                act.wait_ge(ones_set, 1)
                for n in (0, 1):
                    rotated_hi(0, n)
                    rotated_hi(1, n)
                value_hi(0, 0, 8)
                exps(0, 0)

            run(act, ahead, step, lambda: out_hi(LAST, side_count(STEPS, "ot")))

        @block.gpsimd
        def _(pool):
            def rotate(which, n, count_sin):
                pool.wait_ge(side_taken, count_sin + 1)
                pool.tensor_tensor(sin_part[:, which, :], sin_part[:, which, :], four[:, which, :],
                                   ALU.add).then_inc(fourier_added[which], 1)
                pool.wait_ge(fourier_added[which], n + 1)
                pool.tensor_tensor(cos_part[:, which, :], cos_part[:, which, :], sin_part[:, which, :],
                                   ALU.add).then_inc(rotated[which], 1)

            def rotated_lo(which, n):
                pool.wait_ge(rot_hi_ready[which], n + 1)
                pool.tensor_tensor(rot_lo[:, which, :], cos_part[:, which, :], rot_hi[:, which, :],
                                   ALU.subtract).then_inc(rot_split[which], 1)

            def step(g, par):
                if not is_last(g, 2):
                    rotate(0, g + 2, taken_count(g, "qr"))
                    rotated_lo(0, g + 2)
                    rotate(1, g + 2, taken_count(g, "kr"))
                    rotated_lo(1, g + 2)

            def ahead():
                for n in (0, 1):
                    rotate(0, n, 4 * n + 1)
                    rotated_lo(0, n)
                    rotate(1, n, 4 * n + 3)
                    rotated_lo(1, n)

            run(pool, ahead, step, lambda: None)

        @block.vector
        def _(dve):
            def maxima(g, u):
                dve.wait_ge(scores_ready, 4 * g + u + 1)
                at_least(dve, exp_ready, HQ * (4 * g + u - 1))
                dve.tensor_reduce(neg_max[:, u % 2, :], scores[:, u % 2, :, :], AX.X, ALU.max,
                                  negate=True).then_inc(max_ready, 1)

            def probs_lo(g, u):
                dve.wait_ge(pt_hi_ready, 4 * g + u + 1)
                dve.tensor_tensor(pt_lo[:, u % 2, :, :], pt[:], pt_hi[:, u % 2, :, :],
                                  ALU.subtract).then_inc(pt_split, 1)

            def normalise(g, par, u):
                h, half = u // 2, u % 2
                dve.wait_ge(pv_ready, 4 * g + u + 1)
                dve.reciprocal(inv_sum[:, u % 2, :], pv[:, 0:HQ, A_HEAD]).then_inc(inv_ready, 1)
                dve.wait_ge(inv_ready, 4 * g + u + 1)
                dve.tensor_tensor(heads_out[:, par, half * HQ:(half + 1) * HQ, h * A_HEAD:(h + 1) * A_HEAD],
                                  pv[:, 0:HQ, 0:A_HEAD],
                                  inv_sum[:, u % 2, :].unsqueeze(2).to_broadcast([P, HQ, A_HEAD]),
                                  ALU.mult).then_inc(pv_taken, 1)

            def times(which, table, out, n, count):
                dve.wait_ge(side_ready, count + 1)
                at_least(dve, rot_split[which], n)
                dve.tensor_tensor(out[:, which, :], side[:], table[:, which, :], ALU.mult).then_inc(side_taken, 1)

            def value_lo(n, par):
                dve.wait_ge(v_hi_ready, n + 1)
                dve.scalar_tensor_tensor(out=v_lo[:, par, :, :, :], in0=side[:].rearrange("p (a c) -> p a c", c=A_HEAD),
                                         scalar=1.0 / WSCALE, in1=v_hi[:, par, :, :, 0:A_HEAD], op0=ALU.mult,
                                         op1=ALU.subtract).then_inc(v_split, 1)

            def out_lo(p):
                dve.wait_ge(ot_hi_ready, p + 1)
                dve.tensor_tensor(ot_lo[:], side[:], ot_hi[:], ALU.subtract).then_inc(ot_split, 1)

            def add_out(p, count, before):
                dve.wait_ge(side_ready, count + 1)
                dve.wait_ge(side_taken, before)
                x4 = x_all[:, bass.ds(p // A_PAIRS * TPB, TPB), :].rearrange("p t c -> p (t c)")
                dve.scalar_tensor_tensor(out=x4, in0=side[:], scalar=1.0 / WSCALE, in1=x4, op0=ALU.mult,
                                         op1=ALU.add).then_inc(side_taken, 1)

            def before_normalise(g, par, u):
                if u > 0:
                    normalise(g, par, u - 1)
                elif not is_first(g):
                    normalise(g - 1, 1 - par, 3)

            def after_maxima(g, u):
                if not (is_last(g) and u >= 2):
                    maxima(*unit_after(g, u, 2))

            def step(g, par):
                for which, (cos_slot, sin_slot) in enumerate((("q", "qr"), ("k", "kr"))):
                    if not is_last(g, 2):
                        times(which, cos, cos_part, g + 2, side_count(g, cos_slot))
                    probs_lo(g, which)
                    if not is_last(g, 2):
                        times(which, sin, sin_part, g + 2, side_count(g, sin_slot))
                    after_maxima(g, which)
                    before_normalise(g, par, which)
                probs_lo(g, 2)
                if not is_last(g):
                    value_lo(g + 1, 1 - par)
                after_maxima(g, 2)
                before_normalise(g, par, 2)
                if not is_first(g):
                    out_lo(g - 1)
                probs_lo(g, 3)
                after_maxima(g, 3)
                if not is_first(g):
                    add_out(g - 1, side_count(g, "op"), taken_count(g, "end"))
                before_normalise(g, par, 3)

            def ahead():
                dve.memset(v_hi[:], 1.0).then_inc(ones_set, 1)
                for n in (0, 1):
                    for which in (0, 1):
                        times(which, cos, cos_part, n, 4 * n + 2 * which)
                        times(which, sin, sin_part, n, 4 * n + 2 * which + 1)
                value_lo(0, 0)
                maxima(0, 0)
                maxima(0, 1)

            def tail():
                normalise(LAST, LAST % 2, 3)
                out_lo(LAST)
                add_out(LAST, side_count(STEPS, "op"), taken_count(STEPS, "end"))

            run(dve, ahead, step, tail)


def feed_forward_prepare(nc, d, w):
    with ExitStack() as ctx:
        s = Space(nc, ctx, "fp")
        w1_raw = s.sb("w1_raw", [P, HT, DIM], F32)
        w1t_raw = s.sb("w1t_raw", [P, HIDDEN], F32)
        w2t_raw = s.sb("w2t_raw", [P, HT, DIM], F32)
        below = s.sb("below", [P, 2, HIDDEN], F16)
        w2_abs = s.sb("w2_abs", [P, HT, DIM], F32)
        mean_of_rows = s.sb("mean_of_rows", [P, P], F32)
        alpha_bank = s.ps("alpha_bank", [P, SEQ])
        weights_in = s.sem("weights_in")
        masks_ready = s.sem("masks_ready")
        alpha_summed = s.sem("alpha_summed")
        alpha1_sum = s.sem("alpha1_sum")
        done = s.sem("done")
        block = ctx.enter_context(nc.Block())

        @block.sync
        def _(sp):
            for to, name in ((w1_raw, "w1"), (w1t_raw, "w1t"), (w2t_raw, "w2t"), (w["b1"], "b1"), (w["b2"], "b2")):
                sp.dma_start(to[:], d[name]).then_inc(weights_in, 16)
            sp.wait_ge(weights_in, 80)

        @block.vector
        def _(dve):
            dve.memset(mean_of_rows[:], 1.0 / HIDDEN).then_inc(masks_ready, 1)
            dve.wait_ge(weights_in, 80)
            dve.scalar_tensor_tensor(out=w2_abs[:], in0=w2t_raw[:], scalar=-1.0, in1=w2t_raw[:], op0=ALU.mult,
                                     op1=ALU.max).then_inc(masks_ready, 1)
            w2_flat = w2t_raw[:].rearrange("p a c -> p (a c)")
            s2_flat = w["sign2"][:].rearrange("p a c -> p (a c)")
            dve.tensor_scalar(below[:, 0, :], w1t_raw[:], 0.0, None, ALU.is_lt).then_inc(masks_ready, 1)
            dve.tensor_scalar(below[:, 1, :], w2_flat, 0.0, None, ALU.is_lt).then_inc(masks_ready, 1)
            dve.tensor_reduce(w["alpha1"][:], w1_raw[:], AX.X, ALU.add, apply_absolute_value=True).then_inc(alpha1_sum, 1)
            dve.wait_ge(masks_ready, 4)
            dve.scalar_tensor_tensor(out=w["sign1"][:], in0=w1t_raw[:], scalar=0.0, in1=below[:, 0, :],
                                     op0=ALU.is_gt, op1=ALU.subtract).then_inc(done, 1)
            dve.scalar_tensor_tensor(out=s2_flat, in0=w2_flat, scalar=0.0, in1=below[:, 1, :],
                                     op0=ALU.is_gt, op1=ALU.subtract).then_inc(done, 1)
            dve.wait_ge(alpha1_sum, 1)
            dve.tensor_scalar(w["alpha1"][:], w["alpha1"][:], 1.0 / DIM, None, ALU.mult).then_inc(done, 1)
            dve.wait_ge(alpha_summed, 1)
            dve.tensor_copy(w["alpha2"][:], alpha_bank[:, 0:DIM]).then_inc(done, 1)

        @block.tensor
        def _(pe):
            pe.wait_ge(masks_ready, 2)
            for j in range(HT):
                mm = pe.matmul(alpha_bank[:, 0:DIM], mean_of_rows[:], w2_abs[:, j, :], start=(j == 0),
                               stop=(j == HT - 1))
            mm.then_inc(alpha_summed, 1)


def feed_forward(nc, x_all, ident, minus_half, w, tag):
    with ExitStack() as ctx:
        s = Space(nc, ctx, tag)
        xt_hi = s.sb("xt_hi", [P, 2, BLOCK], F16)
        xt_lo = s.sb("xt_lo", [P, 2, BLOCK], F16)
        hidden = s.sb("hidden", [P, 2, HT, BLOCK], F32)
        hidden_hi = s.sb("hidden_hi", [P, 2, HT, BLOCK], F16)
        hidden_lo = s.sb("hidden_lo", [P, 2, HT, BLOCK], F16)
        scaled = s.sb("scaled", [P, TPB, DIM], F32)
        turn_bank = s.ps("turn_bank", [P, BLOCK])
        up = s.ps("up", [P, HT, BLOCK])
        down = s.ps("down", [P, TPB, DIM])
        norm = Norm(s, ident, minus_half, turn_bank)
        up_ready = s.sem("up_ready")
        gelu_ready = s.sem("gelu_ready")
        hidden_hi_ready = s.sem("hidden_hi_ready")
        hidden_split = s.sem("hidden_split")
        down_ready = s.sem("down_ready")
        down_free = s.sem("down_free")
        scaled_ready = s.sem("scaled_ready")
        summed = s.sem("summed")

        def x_block(n):
            if isinstance(n, int):
                return x_all[:, n * TPB:(n + 1) * TPB, :]
            return x_all[:, bass.ds(n * TPB, TPB), :]

        def steps(eng, step):
            with eng.Fori(0, BLOCKS // 2 - 1) as i:
                step(2 * i, 0)
                step(2 * i + 1, 1)
            step(BLOCKS - 2, 0)
            step(BLOCKS - 1, 1)

        def has(n):
            return not isinstance(n, int) or n < BLOCKS

        block = ctx.enter_context(nc.Block())

        @block.tensor
        def _(pe):
            def expand(n, par):
                norm.pe_turn(pe, n)
                pe.wait_ge(norm.xt_ready, n + 1)
                for j in range(HT):
                    if not (isinstance(n, int) and n == 0):
                        pe.wait_ge(gelu_ready, HT * n - HT + j + 1)
                    hid = slice(j * P, (j + 1) * P)
                    pe.matmul(up[:, j, :], w["sign1"][:, hid], xt_hi[:, par, :], start=True, stop=False)
                    pe.matmul(up[:, j, :], w["sign1"][:, hid], xt_lo[:, par, :], start=False,
                              stop=True).then_inc(up_ready, 1)

            def contract(n, par):
                pe.wait_ge(hidden_split, HT * n + HT)
                pe.wait_ge(down_free, n + 1)
                for t in range(TPB):
                    tok = slice(t * P, (t + 1) * P)
                    for j in range(HT):
                        pe.matmul(down[:, t, :], hidden_hi[:, par, j, tok], w["sign2"][:, j, :], start=(j == 0),
                                  stop=False)
                        mm = pe.matmul(down[:, t, :], hidden_lo[:, par, j, tok], w["sign2"][:, j, :], start=False,
                                       stop=(j == HT - 1))
                mm.then_inc(down_ready, 1)

            def step(n, par):
                if has(n + 1):
                    expand(n + 1, 1 - par)
                contract(n, par)

            expand(0, 0)
            steps(pe, step)

        @block.scalar
        def _(act):
            def activate(n, par):
                norm.act_hi(act, n, xt_hi[:, par, :])
                at_least(act, down_free, n)
                for j in range(HT):
                    act.wait_ge(up_ready, HT * n + j + 1)
                    act.activation(hidden[:, par, j, :], up[:, j, :], ACT.Gelu, bias=w["b1"][:, j:j + 1],
                                   scale=w["alpha1"][:, j:j + 1]).then_inc(gelu_ready, 1)
                    act.wait_ge(gelu_ready, HT * n + j + 1)
                    act.activation(hidden_hi[:, par, j, :], hidden[:, par, j, :], ACT.Copy).then_inc(hidden_hi_ready, 1)

            def step(n, par):
                if has(n + 1):
                    activate(n + 1, 1 - par)

            activate(0, 0)
            steps(act, step)

        @block.gpsimd
        def _(pool):
            def split(n, par):
                for j in range(HT):
                    pool.wait_ge(hidden_hi_ready, HT * n + j + 1)
                    pool.tensor_tensor(hidden_lo[:, par, j, :], hidden[:, par, j, :], hidden_hi[:, par, j, :],
                                       ALU.subtract).then_inc(hidden_split, 1)

            def step(n, par):
                if has(n + 2):
                    norm.pool_rstd(pool, n + 2)
                if has(n + 1):
                    split(n + 1, 1 - par)

            norm.pool_rstd(pool, 0)
            norm.pool_rstd(pool, 1)
            split(0, 0)
            steps(pool, step)

        @block.vector
        def _(dve):
            def combine(n):
                x4 = x_block(n)
                dve.wait_ge(summed, n + 1)
                dve.wait_ge(down_ready, n + 1)
                dve.tensor_tensor(scaled[:], down[:], w["alpha2"][:].unsqueeze(1).to_broadcast([P, TPB, DIM]),
                                  ALU.mult).then_inc(down_free, 1)
                dve.tensor_tensor(x4, x4, w["b2"][:].unsqueeze(1).to_broadcast([P, TPB, DIM]),
                                  ALU.add).then_inc(scaled_ready, 1)
                dve.wait_ge(down_free, n + 2)
                dve.wait_ge(scaled_ready, n + 1)
                dve.tensor_tensor(x4, x4, scaled[:], ALU.add).then_inc(summed, 1)

            def lower(n, par):
                norm.dve_lo(dve, n, xt_hi[:, par, :], xt_lo[:, par, :])

            def step(n, par):
                if has(n + 1):
                    lower(n + 1, 1 - par)
                if has(n + 2):
                    norm.dve_moments(dve, n + 2, x_block(n + 2))
                combine(n)
                if has(n + 2):
                    norm.dve_apply(dve, n + 2, x_block(n + 2))

            dve.sem_inc(down_free, 1)
            dve.sem_inc(summed, 1)
            norm.dve_moments(dve, 0, x_block(0))
            norm.dve_apply(dve, 0, x_block(0))
            lower(0, 0)
            norm.dve_moments(dve, 1, x_block(1))
            norm.dve_apply(dve, 1, x_block(1))
            steps(dve, step)


def attention_b_prepare(nc, d, w):
    with ExitStack() as ctx:
        s = Space(nc, ctx, "bp")
        raw = {"k": s.sb("wk_raw", [P, HIDDEN], F32), "q": s.sb("wq_raw", [P, HIDDEN], F32),
               "v": s.sb("wv_raw", [P, DIM], F32), "o": s.sb("wo_raw", [P, DIM], F32)}
        loaded = s.sem("loaded")
        hi_ready = s.sem("hi_ready")
        split = s.sem("split")
        tables = ("bias_k", "bias_q", "bias_v", "bias_o", "lower_rows", "head_rows", "mean_select", "causal", "own_head")
        block = ctx.enter_context(nc.Block())
        LOADS = 16 * (len(raw) + len(tables))

        @block.sync
        def _(sp):
            for name, to in raw.items():
                sp.dma_start(to[:], d[f"w{name}_b"]).then_inc(loaded, 16)
            for name in tables:
                sp.dma_start(w[name][:], d[name]).then_inc(loaded, 16)
            sp.wait_ge(loaded, LOADS)

        @block.scalar
        def _(act):
            act.wait_ge(loaded, LOADS)
            for name, from_ in raw.items():
                act.activation(w[f"{name}_hi"][:], from_[:], ACT.Copy, scale=WSCALE).then_inc(hi_ready, 1)

        @block.vector
        def _(dve):
            for n, (name, from_) in enumerate(raw.items()):
                dve.wait_ge(hi_ready, n + 1)
                dve.scalar_tensor_tensor(out=w[f"{name}_lo"][:], in0=from_[:], scalar=WSCALE, in1=w[f"{name}_hi"][:],
                                         op0=ALU.mult, op1=ALU.subtract).then_inc(split, 1)


def attention_b(nc, x_all, ident, minus_half, w):
    SEQS = BATCH
    UNITS = 2 * CHUNKS
    UH = B_HEADS // 2
    VC = B_HEAD + 1
    INTER = B_HEADS * CHUNKS
    SIDE = ("xt", "k0", "k1", "k2", "k3", "q0", "q1", "q2", "q3", "km", "v", "si", "vm", "ot", "op", "at", "io")
    ACT_TAKES = ("k0", "k1", "k2", "k3", "q0", "q1", "q2", "q3", "io")
    OUTPUT = ("ot", "op")
    with ExitStack() as ctx:
        s = Space(nc, ctx, "b")
        xt_hi = s.sb("xt_hi", [P, SEQ], F16)
        xt_lo = s.sb("xt_lo", [P, SEQ], F16)
        xm = s.sb("xm", [P, CHUNKS], F32)
        xm_hi = s.sb("xm_hi", [P, CHUNKS], F16)
        xm_lo = s.sb("xm_lo", [P, CHUNKS], F16)
        full = s.sb("full", [P, 2, SEQ], F32)
        lower = s.sb("lower", [P, 2, SEQ], F16)
        q_stack = s.sb("q_stack", [P, 2, B_GROUPS, SEQ], F16)
        k_stack = s.sb("k_stack", [P, B_GROUPS, SEQ], F16)
        k_heads = s.sb("k_heads", [P, 2, B_GROUPS, 4, SEQ], F16)
        km_full = s.sb("km_full", [P, B_GROUPS, CHUNKS], F32)
        km_lower = s.sb("km_lower", [P, B_GROUPS, CHUNKS], F16)
        km_stack = s.sb("km_stack", [P, B_GROUPS, CHUNKS], F16)
        km_heads = s.sb("km_heads", [P, B_GROUPS, 4, CHUNKS], F16)
        v_full = s.sb("v_full", [P, CHUNKS, DIM], F32)
        v_hi = s.sb("v_hi", [P, 2, CHUNKS, B_HEADS, VC], F16)
        v_lo = s.sb("v_lo", [P, 2, CHUNKS, B_HEADS, B_HEAD], F16)
        vm_full = s.sb("vm_full", [INTER, DIM], F32)
        vm_hi = s.sb("vm_hi", [INTER, DIM], F16)
        vm_lo = s.sb("vm_lo", [INTER, DIM], F16)
        inter = s.sb("inter", [P, CHUNKS * INTER], F32)
        inter_max = s.sb("inter_max", [P, INTER], F32)
        inter_exp = s.sb("inter_exp", [P, CHUNKS * INTER], F32)
        inter_sum = s.sb("inter_sum", [P, INTER], F32)
        inter_inv = s.sb("inter_inv", [P, INTER], F32)
        inter_probs = s.sb("inter_probs", [P, CHUNKS + 1, INTER], F32)
        at_hi = s.sb("at_hi", [INTER, SEQ], F16)
        at_lo = s.sb("at_lo", [INTER, SEQ], F16)
        inter_out = s.sb("inter_out", [P, 2, CHUNKS, DIM], F32)
        maxes = s.sb("maxes", [P, 2, UH], F32)
        shifted = s.sb("shifted", [P, 2, UH, CHUNK], F32)
        probs = s.sb("probs", [P, 2, UH, CHUNK], F32)
        pt_hi = s.sb("pt_hi", [P, 2, UH, CHUNK], F16)
        pt_lo = s.sb("pt_lo", [P, 2, UH, CHUNK], F16)
        inv_sum = s.sb("inv_sum", [P, UH], F32)
        intra_out = s.sb("intra_out", [P, UH, B_HEAD], F32)
        heads_out = s.sb("heads_out", [P, 2, CHUNKS, DIM], F32)
        ot_hi = s.sb("ot_hi", [P, SEQ], F16)
        ot_lo = s.sb("ot_lo", [P, SEQ], F16)
        scores = s.ps("scores", [P, 2, UH, CHUNK])
        pt = s.ps("pt", [P, UH, CHUNK])
        pv = s.ps("pv", [P, UH, 64])
        side = s.ps("side", [P, SEQ])
        norm = Norm(s, ident, minus_half, side)
        side_ready = s.sem("side_ready")
        dve_took = s.sem("dve_took")
        act_took = s.sem("act_took")
        scores_ready = s.sem("scores_ready")
        max_ready = s.sem("max_ready")
        shift_ready = s.sem("shift_ready")
        exp_ready = s.sem("exp_ready")
        pt_ready = s.sem("pt_ready")
        pt_hi_ready = s.sem("pt_hi_ready")
        pt_split = s.sem("pt_split")
        pv_ready = s.sem("pv_ready")
        inv_ready = s.sem("inv_ready")
        intra_ready = s.sem("intra_ready")
        out_ready = s.sem("out_ready")
        xm_sum = s.sem("xm_sum")
        xm_split = s.sem("xm_split")
        lower_ready = s.sem("lower_ready")
        stack_ready = s.sem("stack_ready")
        k_heads_ready = s.sem("k_heads_ready")
        km_steps = s.sem("km_steps")
        v_hi_ready = s.sem("v_hi_ready")
        v_split = s.sem("v_split")
        vm_steps = s.sem("vm_steps")
        inter_steps = s.sem("inter_steps")
        inter_exp_ready = s.sem("inter_exp_ready")
        at_hi_ready = s.sem("at_hi_ready")
        ot_hi_ready = s.sem("ot_hi_ready")
        bias_added = s.sem("bias_added")
        ones_set = s.sem("ones_set")

        def uses(n_or_b, item):
            t = n_or_b + 1 if item in OUTPUT else n_or_b
            short = [i for i in SIDE if i not in OUTPUT]
            kinds = lambda items: (len(items), sum(i not in ACT_TAKES for i in items), sum(i in ACT_TAKES for i in items))
            if not isinstance(t, int):
                before, per = kinds(SIDE[:SIDE.index(item)]), kinds(SIDE)
                ahead = kinds(short)
                t_ = n_or_b + 2 if item in OUTPUT else n_or_b
                return tuple(2 * a + p * (t_ - 2) + x for a, p, x in zip(ahead, per, before))
            t_ = n_or_b + 2 if item in OUTPUT else n_or_b
            if t_ < 2:
                done = short * t_ + short[:short.index(item)]
            elif t_ < SEQS:
                done = short * 2 + list(SIDE) * (t_ - 2) + list(SIDE[:SIDE.index(item)])
            else:
                done = short * 2 + list(SIDE) * (SEQS - 2) + list(OUTPUT) * (t_ - SEQS) + list(OUTPUT[:OUTPUT.index(item)])
            return kinds(done)

        def all_of(n_or_b, item):
            return uses(n_or_b, item)[0]

        def is_last(b):
            return isinstance(b, int) and b == SEQS - 1

        def is_first(b):
            return isinstance(b, int) and b == 0

        def run(eng, ahead, step, tail):
            ahead()
            step(0, 0)
            with eng.Fori(0, (SEQS - 4) // 2) as i:
                step(2 * i + 1, 1)
                step(2 * i + 2, 0)
            for b in range(SEQS - 3, SEQS):
                step(b, b % 2)
            tail()

        def unit_after(b, u, ahead):
            return b + (u + ahead) // UNITS, (u + ahead) % UNITS

        def x_block(n):
            if isinstance(n, int):
                return x_all[:, n * TPB:(n + 1) * TPB, :]
            return x_all[:, bass.ds(n * TPB, TPB), :]

        block = ctx.enter_context(nc.Block())

        @block.tensor
        def _(pe):
            def bank_free(n, item):
                _, by_dve, by_act = uses(n, item)
                at_least(pe, dve_took, by_dve)
                at_least(pe, act_took, by_act)

            def turn_x(n):
                bank_free(n, "xt")
                pe.wait_ge(norm.normed_ready, TPB * n + TPB)
                for t in range(TPB):
                    mm = pe.transpose(side[:, t * P:(t + 1) * P], norm.normed[:, t, :], ident[:])
                mm.then_inc(side_ready, 1)

            def project(name, g, n):
                bank_free(n, f"{name}{g}")
                rows = slice(g * P, (g + 1) * P)
                three_products(pe, side[:], w[f"{name}_hi"][:, rows], w[f"{name}_lo"][:, rows], xt_hi[:],
                               xt_lo[:]).then_inc(side_ready, 1)

            def key_means(n):
                bank_free(n, "km")
                pe.wait_ge(xm_split, 2 * n + 2)
                for g in range(B_GROUPS):
                    rows = slice(g * P, (g + 1) * P)
                    mm = three_products(pe, side[:, g * CHUNKS:(g + 1) * CHUNKS], w["k_hi"][:, rows],
                                        w["k_lo"][:, rows], xm_hi[:], xm_lo[:])
                mm.then_inc(side_ready, 1)

            def project_v(n):
                bank_free(n, "v")
                for c in range(CHUNKS):
                    tok = slice(c * P, (c + 1) * P)
                    mm = three_products(pe, side[:, tok], xt_hi[:, tok], xt_lo[:, tok], w["v_hi"][:], w["v_lo"][:])
                mm.then_inc(side_ready, 1)

            def inter_scores(n, par):
                bank_free(n, "si")
                pe.wait_ge(stack_ready, 8 * n + 8)
                pe.wait_ge(km_steps, 6 * n + 6)
                for c in range(CHUNKS):
                    for g in range(B_GROUPS):
                        at = (c * B_GROUPS + g) * 16
                        mm = pe.matmul(side[:, at:at + 16], q_stack[:, par, g, c * P:(c + 1) * P],
                                       km_heads[:, g, :, :], start=True, stop=True)
                mm.then_inc(side_ready, 1)

            def value_means(n, par):
                bank_free(n, "vm")
                pe.wait_ge(v_split, n + 1)
                for c in range(CHUNKS):
                    pe.matmul(side[0:INTER, 0:DIM], w["mean_select"][:, c, :], v_hi[:, par, c, :, 0:B_HEAD],
                              start=(c == 0), stop=False)
                    mm = pe.matmul(side[0:INTER, 0:DIM], w["mean_select"][:, c, :], v_lo[:, par, c, :, :],
                                   start=False, stop=(c == CHUNKS - 1))
                mm.then_inc(side_ready, 1)

            def turn_inter(n):
                bank_free(n, "at")
                pe.wait_ge(ones_set, 2)
                pe.wait_ge(inter_steps, 5 * n + 5)
                for c in range(CHUNKS):
                    mm = pe.transpose(side[:, c * P:(c + 1) * P],
                                      inter_probs[:, c:c + 2, :].rearrange("p c i -> p (c i)"), ident[:])
                mm.then_inc(side_ready, 1)

            def inter_product(n):
                bank_free(n, "io")
                pe.wait_ge(vm_steps, 2 * n + 2)
                for c in range(CHUNKS):
                    tok = slice(c * P, (c + 1) * P)
                    mm = three_products(pe, side[:, tok], at_hi[:, tok], at_lo[:, tok], vm_hi[:], vm_lo[:])
                mm.then_inc(side_ready, 1)

            def turn_out(p, par):
                bank_free(p, "ot")
                pe.wait_ge(out_ready, UNITS * p + UNITS)
                for c in range(CHUNKS):
                    mm = pe.transpose(side[:, c * P:(c + 1) * P], heads_out[:, par, c, :], ident[:])
                mm.then_inc(side_ready, 1)

            def project_out(p):
                bank_free(p, "op")
                for c in range(CHUNKS):
                    tok = slice(c * P, (c + 1) * P)
                    mm = three_products(pe, side[:, tok], ot_hi[:, tok], ot_lo[:, tok], w["o_hi"][:], w["o_lo"][:])
                mm.then_inc(side_ready, 1)

            def score(b, par, u):
                c, half = u // 2, u % 2
                if u == 0:
                    pe.wait_ge(stack_ready, 8 * b + 8)
                    pe.wait_ge(k_heads_ready, 4 * b + 4)
                at_least(pe, shift_ready, UNITS * b + u - 1)
                for j in range(2):
                    g = 2 * half + j
                    mm = pe.matmul(scores[:, u % 2, 4 * j:4 * j + 4, :], q_stack[:, par, g, c * P:(c + 1) * P],
                                   k_heads[:, par, g, :, c * P:(c + 1) * P], start=True, stop=True)
                mm.then_inc(scores_ready, 1)

            def turn(b, u):
                pe.wait_ge(exp_ready, UNITS * b + u + 1)
                at_least(pe, pt_split, UNITS * b + u)
                for h in range(UH):
                    mm = pe.transpose(pt[:, h, :], probs[:, u % 2, h, :], ident[:])
                mm.then_inc(pt_ready, 1)

            def values(b, par, u):
                c, half = u // 2, u % 2
                if u == 0:
                    pe.wait_ge(v_split, b + 1)
                pe.wait_ge(pt_split, UNITS * b + u + 1)
                at_least(pe, intra_ready, UNITS * b + u)
                for h in range(UH):
                    hh = UH * half + h
                    p_hi, p_lo = pt_hi[:, u % 2, h, :], pt_lo[:, u % 2, h, :]
                    pe.matmul(pv[:, h, 0:VC], p_hi, v_hi[:, par, c, hh, :], start=True, stop=False)
                    pe.matmul(pv[:, h, 0:B_HEAD], p_hi, v_lo[:, par, c, hh, :], start=False, stop=False)
                    mm = pe.matmul(pv[:, h, 0:VC], p_lo, v_hi[:, par, c, hh, :], start=False, stop=True)
                mm.then_inc(pv_ready, 1)

            def step(b, par):
                nxt = 1 - par
                none = lambda: None
                first_of = (lambda: turn_x(b + 1), lambda: project("k", 1, b + 1), lambda: project("k", 3, b + 1),
                            lambda: project("q", 1, b + 1), lambda: project("q", 3, b + 1),
                            lambda: project_v(b + 1), lambda: value_means(b + 1, nxt), none)
                second_of = (lambda: project("k", 0, b + 1), lambda: project("k", 2, b + 1),
                             lambda: project("q", 0, b + 1), lambda: project("q", 2, b + 1),
                             lambda: key_means(b + 1), lambda: inter_scores(b + 1, nxt), none,
                             lambda: turn_inter(b + 1))
                for u in range(UNITS):
                    turn(b, u)
                    if not is_last(b):
                        first_of[u]()
                    if u == 7 and not is_first(b):
                        project_out(b - 1)
                    b2, u2 = unit_after(b, u, 2)
                    if not (is_last(b) and u >= UNITS - 2):
                        score(b2, par if u < UNITS - 2 else nxt, u2)
                    if not is_last(b):
                        second_of[u]()
                    if u == 6 and not is_first(b):
                        turn_out(b - 1, nxt)
                    if u > 0:
                        values(b, par, u - 1)
                    elif not is_first(b):
                        values(b - 1, nxt, UNITS - 1)
                if not is_last(b):
                    inter_product(b + 1)

            def ahead():
                turn_x(0)
                for name in ("k", "q"):
                    for g in range(B_GROUPS):
                        project(name, g, 0)
                key_means(0)
                project_v(0)
                inter_scores(0, 0)
                value_means(0, 0)
                turn_inter(0)
                inter_product(0)
                score(0, 0, 0)
                score(0, 0, 1)

            def tail():
                values(SEQS - 1, 1, UNITS - 1)
                turn_out(SEQS - 1, 1)
                project_out(SEQS - 1)

            run(pe, ahead, step, tail)

        @block.scalar
        def _(act):
            def x_hi(n):
                act.wait_ge(side_ready, all_of(n, "xt") + 1)
                act.activation(xt_hi[:], side[:], ACT.Copy).then_inc(norm.hi_ready, 1)

            def biased(name, g, n):
                i = g + (0 if name == "k" else B_GROUPS)
                act.wait_ge(side_ready, all_of(n, f"{name}{g}") + 1)
                at_least(act, stack_ready, 8 * n + i - 1)
                act.activation(full[:, i % 2, :], side[:], ACT.Identity, bias=w[f"bias_{name}"][:, g:g + 1],
                               scale=1.0 / WSCALE).then_inc(act_took, 1)
                act.wait_ge(act_took, uses(n, f"{name}{g}")[2] + 1)
                rows = w["lower_rows"][:, (0 if name == "k" else 1):(1 if name == "k" else 2)]
                act.activation(lower[:, i % 2, :], full[:, i % 2, :], ACT.Copy, scale=rows).then_inc(lower_ready, 1)

            def inter_exps(n):
                act.wait_ge(inter_steps, 5 * n + 2)
                act.activation(inter_exp[:], inter[:], ACT.Exp, scale=B_SCALE).then_inc(inter_exp_ready, 1)

            def inter_hi(n):
                act.wait_ge(side_ready, all_of(n, "at") + 1)
                act.activation(at_hi[:], side[0:INTER, :], ACT.Copy).then_inc(at_hi_ready, 1)

            def inter_copy(n, par):
                act.wait_ge(side_ready, all_of(n, "io") + 1)
                act.activation(inter_out[:, par, :, :].rearrange("p c f -> p (c f)"), side[:],
                               ACT.Copy).then_inc(act_took, 1)

            def out_hi(p):
                act.wait_ge(side_ready, all_of(p, "ot") + 1)
                act.activation(ot_hi[:], side[:], ACT.Copy).then_inc(ot_hi_ready, 1)

            def value_hi(n, par):
                act.wait_ge(dve_took, uses(n, "v")[1] + 1)
                at_least(act, pv_ready, UNITS * (n - 1))
                act.activation(v_hi[:, par, :, :, 0:B_HEAD],
                               v_full[:].rearrange("p c (h e) -> p c h e", h=B_HEADS),
                               ACT.Copy).then_inc(v_hi_ready, 1)

            def exps(b, u):
                act.wait_ge(shift_ready, UNITS * b + u + 1)
                at_least(act, pt_ready, UNITS * b + u - 1)
                act.activation(probs[:, u % 2, :, :], shifted[:, u % 2, :, :], ACT.Exp,
                               scale=B_SCALE).then_inc(exp_ready, 1)

            def probs_hi(b, u):
                act.wait_ge(pt_ready, UNITS * b + u + 1)
                at_least(act, pv_ready, UNITS * b + u - 1)
                act.activation(pt_hi[:, u % 2, :, :], pt[:], ACT.Copy).then_inc(pt_hi_ready, 1)

            def step(b, par):
                nxt = 1 - par
                n = b + 1
                none = lambda: None
                early = (lambda: x_hi(n), lambda: biased("k", 1, n), lambda: biased("k", 3, n),
                         lambda: biased("q", 1, n), lambda: biased("q", 3, n), none, none, none)
                late = (lambda: biased("k", 0, n), lambda: biased("k", 2, n), lambda: biased("q", 0, n),
                        lambda: biased("q", 2, n), none, lambda: value_hi(n, nxt), lambda: inter_exps(n),
                        lambda: inter_hi(n))
                for u in range(UNITS):
                    probs_hi(b, u)
                    if not is_last(b):
                        early[u]()
                    if not (is_last(b) and u == UNITS - 1):
                        exps(*unit_after(b, u, 1))
                    if not is_last(b):
                        late[u]()
                    if u == 6 and not is_first(b):
                        out_hi(b - 1)
                if not is_last(b):
                    inter_copy(n, nxt)

            def ahead():
                act.wait_ge(ones_set, 1)
                x_hi(0)
                for name in ("k", "q"):
                    for g in range(B_GROUPS):
                        biased(name, g, 0)
                value_hi(0, 0)
                inter_exps(0)
                inter_hi(0)
                inter_copy(0, 0)
                exps(0, 0)

            run(act, ahead, step, lambda: out_hi(SEQS - 1))

        @block.gpsimd
        def _(pool):
            def add_bias(n):
                pool.wait_ge(norm.normed_ready, TPB * n + TPB)
                x4 = x_block(n)
                pool.tensor_tensor(x4, x4, w["bias_o"][:].unsqueeze(1).to_broadcast([P, TPB, DIM]),
                                   ALU.add).then_inc(bias_added, 1)

            def stack(name, g, n, par):
                i = g + (0 if name == "k" else B_GROUPS)
                pool.wait_ge(lower_ready, 8 * n + i + 1)
                if name == "k":
                    at_least(pool, k_heads_ready, 4 * n)
                    to = k_stack[:, g, :]
                else:
                    at_least(pool, scores_ready, UNITS * (n - 1))
                    to = q_stack[:, par, g, :]
                pool.tensor_tensor(to, full[:, i % 2, :], lower[:, i % 2, :], ALU.subtract).then_inc(stack_ready, 1)

            def step(b, par):
                n = b + 1
                if not is_last(b):
                    add_bias(n)
                    for g in range(B_GROUPS):
                        stack("k", g, n, 1 - par)
                    if not (isinstance(b, int) and b >= SEQS - 2):
                        norm.pool_rstd(pool, b + 2)
                    for g in range(B_GROUPS):
                        stack("q", g, n, 1 - par)

            def ahead():
                norm.pool_rstd(pool, 0)
                add_bias(0)
                for name in ("k", "q"):
                    for g in range(B_GROUPS):
                        stack(name, g, 0, 0)
                norm.pool_rstd(pool, 1)

            run(pool, ahead, step, lambda: None)

        @block.vector
        def _(dve):
            def x_lo_and_sums(n):
                dve.wait_ge(norm.hi_ready, n + 1)
                dve.tensor_tensor(xt_lo[:], side[:], xt_hi[:], ALU.subtract).then_inc(norm.xt_ready, 1)
                dve.tensor_reduce(xm[:], side[:].rearrange("p (c t) -> p c t", c=CHUNKS), AX.X,
                                  ALU.add).then_inc(dve_took, 1)

            def x_means(n):
                dve.wait_ge(dve_took, uses(n, "xt")[1] + 1)
                dve.tensor_scalar(xm_hi[:], xm[:], 1.0 / CHUNK, None, ALU.mult).then_inc(xm_split, 1)
                dve.wait_ge(xm_split, 2 * n + 1)
                dve.scalar_tensor_tensor(out=xm_lo[:], in0=xm[:], scalar=1.0 / CHUNK, in1=xm_hi[:], op0=ALU.mult,
                                         op1=ALU.subtract).then_inc(xm_split, 1)

            def heads_of_k(n, par):
                dve.wait_ge(stack_ready, 8 * n + B_GROUPS)
                if not is_first(n):
                    at_least(dve, scores_ready, UNITS * (n - 1))
                for r in range(4):
                    dve.tensor_scalar(k_heads[:, par, :, r, :], k_stack[:], w["head_rows"][:, r:r + 1], None,
                                      ALU.mult).then_inc(k_heads_ready, 1)

            def means_of_k(n):
                dve.wait_ge(side_ready, all_of(n, "km") + 1)
                flat = lambda t: t[:].rearrange("p g c -> p (g c)")
                dve.scalar_tensor_tensor(out=km_full[:], in0=side[:, 0:B_GROUPS * CHUNKS].rearrange(
                    "p (g c) -> p g c", g=B_GROUPS), scalar=1.0 / WSCALE,
                    in1=w["bias_k"][:].unsqueeze(2).to_broadcast([P, B_GROUPS, CHUNKS]), op0=ALU.mult,
                    op1=ALU.add).then_inc(dve_took, 1)
                dve.wait_ge(dve_took, uses(n, "km")[1] + 1)
                dve.tensor_scalar(flat(km_lower), flat(km_full), w["lower_rows"][:, 0:1], None,
                                  ALU.mult).then_inc(km_steps, 1)
                dve.wait_ge(km_steps, 6 * n + 1)
                dve.tensor_tensor(flat(km_stack), flat(km_full), flat(km_lower), ALU.subtract).then_inc(km_steps, 1)
                dve.wait_ge(km_steps, 6 * n + 2)
                for r in range(4):
                    dve.tensor_scalar(km_heads[:, :, r, :], km_stack[:], w["head_rows"][:, r:r + 1], None,
                                      ALU.mult).then_inc(km_steps, 1)

            def value_full(n):
                dve.wait_ge(side_ready, all_of(n, "v") + 1)
                if not is_first(n):
                    dve.wait_ge(v_split, n)
                dve.scalar_tensor_tensor(out=v_full[:], in0=side[:].rearrange("p (c f) -> p c f", c=CHUNKS),
                                         scalar=1.0 / WSCALE,
                                         in1=w["bias_v"][:].unsqueeze(1).to_broadcast([P, CHUNKS, DIM]),
                                         op0=ALU.mult, op1=ALU.add).then_inc(dve_took, 1)

            def value_lo(n, par):
                dve.wait_ge(v_hi_ready, n + 1)
                dve.tensor_tensor(v_lo[:, par, :, :, :].rearrange("p c h e -> p (c h) e"),
                                  v_full[:].rearrange("p c (h e) -> p (c h) e", h=B_HEADS),
                                  v_hi[:, par, :, :, 0:B_HEAD].rearrange("p c h e -> p (c h) e"),
                                  ALU.subtract).then_inc(v_split, 1)

            def inter_shift(n):
                dve.wait_ge(side_ready, all_of(n, "si") + 1)
                quads = lambda t: t[:].rearrange("p (i j) -> p i j", j=CHUNKS)
                if not is_first(n):
                    dve.wait_ge(inter_exp_ready, n)
                dve.tensor_tensor(inter[:], side[:, 0:CHUNKS * INTER], w["causal"][:], ALU.add).then_inc(dve_took, 1)
                dve.wait_ge(dve_took, uses(n, "si")[1] + 1)
                dve.tensor_reduce(inter_max[:], quads(inter), AX.X, ALU.max).then_inc(inter_steps, 1)
                dve.wait_ge(inter_steps, 5 * n + 1)
                dve.tensor_tensor(quads(inter), quads(inter),
                                  inter_max[:].unsqueeze(2).to_broadcast([P, INTER, CHUNKS]),
                                  ALU.subtract).then_inc(inter_steps, 1)

            def inter_normalise(n):
                quads = lambda t: t[:].rearrange("p (i j) -> p i j", j=CHUNKS)
                dve.wait_ge(inter_exp_ready, n + 1)
                dve.tensor_reduce(inter_sum[:], quads(inter_exp), AX.X, ALU.add).then_inc(inter_steps, 1)
                dve.wait_ge(inter_steps, 5 * n + 3)
                dve.reciprocal(inter_inv[:], inter_sum[:]).then_inc(inter_steps, 1)
                dve.wait_ge(inter_steps, 5 * n + 4)
                dve.tensor_tensor(inter_probs[:, 0:CHUNKS, :].rearrange("p c (i j) -> p (c i) j", j=CHUNKS), quads(inter_exp),
                                  inter_inv[:].unsqueeze(2).to_broadcast([P, INTER, CHUNKS]),
                                  ALU.mult).then_inc(inter_steps, 1)

            def means_of_v(n):
                dve.wait_ge(side_ready, all_of(n, "vm") + 1)
                if not is_first(n):
                    dve.wait_ge(act_took, uses(n - 1, "io")[2] + 1)
                dve.tensor_tensor(vm_full[:], side[0:INTER, 0:DIM], w["own_head"][:], ALU.mult).then_inc(dve_took, 1)
                dve.wait_ge(dve_took, uses(n, "vm")[1] + 1)
                dve.tensor_copy(vm_hi[:], vm_full[:]).then_inc(vm_steps, 1)
                dve.wait_ge(vm_steps, 2 * n + 1)
                dve.tensor_tensor(vm_lo[:], vm_full[:], vm_hi[:], ALU.subtract).then_inc(vm_steps, 1)

            def inter_lo(n):
                dve.wait_ge(at_hi_ready, n + 1)
                dve.tensor_tensor(at_lo[:], side[0:INTER, :], at_hi[:], ALU.subtract).then_inc(dve_took, 1)

            def out_lo(p):
                dve.wait_ge(ot_hi_ready, p + 1)
                dve.tensor_tensor(ot_lo[:], side[:], ot_hi[:], ALU.subtract).then_inc(dve_took, 1)

            def add_out(p):
                dve.wait_ge(side_ready, all_of(p, "op") + 1)
                dve.wait_ge(bias_added, p + 1)
                x4 = x_block(p)
                dve.scalar_tensor_tensor(out=x4, in0=side[:].rearrange("p (t f) -> p t f", t=TPB),
                                         scalar=1.0 / WSCALE, in1=x4, op0=ALU.mult, op1=ALU.add).then_inc(dve_took, 1)

            def maxima(b, u):
                dve.wait_ge(scores_ready, UNITS * b + u + 1)
                dve.tensor_reduce(maxes[:, u % 2, :], scores[:, u % 2, :, :], AX.X, ALU.max).then_inc(max_ready, 1)

            def shift(b, u):
                dve.wait_ge(max_ready, UNITS * b + u + 1)
                at_least(dve, exp_ready, UNITS * b + u - 1)
                dve.tensor_tensor(shifted[:, u % 2, :, :], scores[:, u % 2, :, :],
                                  maxes[:, u % 2, :].unsqueeze(2).to_broadcast([P, UH, CHUNK]),
                                  ALU.subtract).then_inc(shift_ready, 1)

            def probs_lo(b, u):
                dve.wait_ge(pt_hi_ready, UNITS * b + u + 1)
                dve.tensor_tensor(pt_lo[:, u % 2, :, :], pt[:], pt_hi[:, u % 2, :, :],
                                  ALU.subtract).then_inc(pt_split, 1)

            def normalise(b, par, u):
                c, half = u // 2, u % 2
                dve.wait_ge(pv_ready, UNITS * b + u + 1)
                dve.reciprocal(inv_sum[:], pv[:, :, B_HEAD]).then_inc(inv_ready, 1)
                dve.wait_ge(inv_ready, UNITS * b + u + 1)
                dve.tensor_tensor(intra_out[:], pv[:, :, 0:B_HEAD], inv_sum[:].unsqueeze(2).to_broadcast([P, UH, B_HEAD]),
                                  ALU.mult).then_inc(intra_ready, 1)
                dve.wait_ge(intra_ready, UNITS * b + u + 1)
                if u == 0:
                    dve.wait_ge(act_took, uses(b, "io")[2] + 1)
                cols = slice(half * UH * B_HEAD, (half + 1) * UH * B_HEAD)
                dve.tensor_tensor(heads_out[:, par, c, cols], intra_out[:].rearrange("p h e -> p (h e)"),
                                  inter_out[:, par, c, cols], ALU.add).then_inc(out_ready, 1)

            def step(b, par):
                nxt, n = 1 - par, b + 1
                none = lambda: None
                early = (none, none, none, none, lambda: heads_of_k(n, nxt), lambda: value_full(n), none, none)
                late = (none, none, none, none, lambda: means_of_k(n),
                        lambda: (value_lo(n, nxt), inter_shift(n)), lambda: means_of_v(n),
                        lambda: (inter_normalise(n), inter_lo(n)))
                for u in range(UNITS):
                    if u == 7 and not is_first(b):
                        out_lo(b - 1)
                    if u == 0 and not is_last(b):
                        x_lo_and_sums(n)
                    probs_lo(b, u)
                    if u == 0 and not is_last(b):
                        x_means(n)
                    if not is_last(b):
                        early[u]()
                    b2, u2 = unit_after(b, u, 2)
                    if not (is_last(b) and u >= UNITS - 2):
                        maxima(b2, u2)
                        shift(b2, u2)
                    if u == 7 and not is_first(b):
                        add_out(b - 1)
                    if not is_last(b):
                        late[u]()
                    if u > 0:
                        normalise(b, par, u - 1)
                    elif not is_first(b):
                        normalise(b - 1, nxt, UNITS - 1)
                    if not (isinstance(b, int) and b >= SEQS - 2):
                        if u == 1:
                            norm.dve_moments(dve, b + 2, x_block(b + 2))
                        if u == 4:
                            norm.dve_apply(dve, b + 2, x_block(b + 2))

            def ahead():
                dve.memset(v_hi[:], 1.0).then_inc(ones_set, 1)
                dve.memset(inter_probs[:, CHUNKS, :], 0.0).then_inc(ones_set, 1)
                norm.dve_moments(dve, 0, x_block(0))
                norm.dve_apply(dve, 0, x_block(0))
                x_lo_and_sums(0)
                x_means(0)
                norm.dve_moments(dve, 1, x_block(1))
                norm.dve_apply(dve, 1, x_block(1))
                heads_of_k(0, 0)
                means_of_k(0)
                value_full(0)
                value_lo(0, 0)
                inter_shift(0)
                means_of_v(0)
                inter_normalise(0)
                inter_lo(0)
                maxima(0, 0)
                shift(0, 0)
                maxima(0, 1)
                shift(0, 1)

            def tail():
                normalise(SEQS - 1, 1, UNITS - 1)
                out_lo(SEQS - 1)
                add_out(SEQS - 1)

            run(dve, ahead, step, tail)


def program(nc, d, out):
    with ExitStack() as ctx:
        s = Space(nc, ctx, "m")
        x_all = s.sb("x_all", [P, TILES, DIM], F32)
        ident = s.sb("ident", [P, P], F32)
        minus_half = s.sb("minus_half", [P, TPB], F32)
        w = {"sign1": s.sb("sign1", [P, HIDDEN], F16), "sign2": s.sb("sign2", [P, HT, DIM], F16),
             "alpha1": s.sb("alpha1", [P, HT], F32), "alpha2": s.sb("alpha2", [P, DIM], F32),
             "b1": s.sb("b1", [P, HT], F32), "b2": s.sb("b2", [P, DIM], F32)}
        attention_a(nc, d, x_all, ident, minus_half)
        feed_forward_prepare(nc, d, w)
        feed_forward(nc, x_all, ident, minus_half, w, "f1")
        with ExitStack() as keep:
            sb = Space(nc, keep, "bw")
            wb = {"k_hi": sb.sb("k_hi", [P, HIDDEN], F16), "k_lo": sb.sb("k_lo", [P, HIDDEN], F16),
                  "q_hi": sb.sb("q_hi", [P, HIDDEN], F16), "q_lo": sb.sb("q_lo", [P, HIDDEN], F16),
                  "v_hi": sb.sb("v_hi", [P, DIM], F16), "v_lo": sb.sb("v_lo", [P, DIM], F16),
                  "o_hi": sb.sb("o_hi", [P, DIM], F16), "o_lo": sb.sb("o_lo", [P, DIM], F16),
                  "bias_k": sb.sb("bias_k", [P, B_GROUPS], F32), "bias_q": sb.sb("bias_q", [P, B_GROUPS], F32),
                  "bias_v": sb.sb("bias_v", [P, DIM], F32), "bias_o": sb.sb("bias_o", [P, DIM], F32),
                  "lower_rows": sb.sb("lower_rows", [P, 2], F32), "head_rows": sb.sb("head_rows", [P, 4], F32),
                  "mean_select": sb.sb("mean_select", [P, CHUNKS, B_HEADS * CHUNKS], F16),
                  "causal": sb.sb("causal", [P, CHUNKS * B_HEADS * CHUNKS], F32),
                  "own_head": sb.sb("own_head", [B_HEADS * CHUNKS, DIM], F32)}
            attention_b_prepare(nc, d, wb)
            attention_b(nc, x_all, ident, minus_half, wb)
        feed_forward(nc, x_all, ident, minus_half, w, "f2")
        x_out = s.sem("x_out")
        with nc.Block() as block:
            @block.sync
            def _(sp):
                sp.dma_start(out, x_all[:]).then_inc(x_out, 16)
                sp.wait_ge(x_out, 16)


def layouts(a):
    f = {k[3:]: np.ascontiguousarray(v) for k, v in a.items()}
    d = {}
    d["x"] = f["attn_a_x"].reshape(TILES, P, DIM).transpose(1, 0, 2)
    wq, wk, wv = f["attn_a_w_qkv"].reshape(3, A_HEADS, A_HEAD, DIM)
    order = np.concatenate([np.arange(1, A_HEAD, 2), np.arange(0, A_HEAD, 2)])
    kinds = [wq, wq[:, order], wk, wk[:, order], wv]
    d["w_a"] = np.stack([w.reshape(A_INNER, DIM).T for w in kinds], axis=1)
    d["wo_a"] = f["attn_a_w_out"].T.reshape(A_PAIRS, P, DIM).transpose(1, 0, 2)
    d["b_out_a"] = np.broadcast_to(f["attn_a_b_out"], (P, DIM))
    d["w_four"] = np.tile(f["attn_a_w_fproj"].T, (1, 2))
    d["b_four"] = np.tile(f["attn_a_b_fproj"], 2)[:, None]
    pos = np.arange(SEQ, dtype=np.float32)[:, None]
    freqs = np.float32(10000.0) ** (-np.arange(0, A_HEAD, 2, dtype=np.float32) / np.float32(A_HEAD))
    angles = pos * freqs
    sign = np.where(np.arange(A_HEAD) < A_HEAD // 2, -1.0, 1.0)[:, None]
    cos = np.repeat(np.cos(angles), 2, axis=1).T
    sin = np.repeat(np.sin(angles), 2, axis=1).T * sign
    scales = np.array([A_SCALE, 1.0])[:, None, None] / WSCALE
    d["cos"] = (np.tile(cos, (2, 1))[None] * scales).astype(np.float32)
    d["sin"] = (np.tile(sin, (2, 1))[None] * scales).astype(np.float32)
    harmonics = pos * np.arange(1, FREQS + 1, dtype=np.float32)
    d["fourier"] = np.concatenate([np.sin(harmonics), np.cos(harmonics)], axis=-1).T
    d["ident"] = np.eye(P, dtype=np.float32)
    w1, w2 = f["ffn_w1"], f["ffn_w2"]
    d["w1"] = w1.reshape(HT, P, DIM).transpose(1, 0, 2)
    d["w1t"] = w1.T
    d["w2t"] = w2.T.reshape(HT, P, DIM).transpose(1, 0, 2)
    d["b1"] = f["ffn_b1"].reshape(HT, P).T
    d["b2"] = np.broadcast_to(f["ffn_b2"], (P, DIM))

    def stacked(t):
        t = t.reshape(B_GROUPS, 4, 1, B_HEAD, -1)
        return np.concatenate([t, t, t, np.zeros_like(t)], axis=2).reshape(HIDDEN, -1)

    for name in "qk":
        d[f"w{name}_b"] = stacked(f[f"attn_b_w{name}"]).T
        d[f"bias_{name}"] = stacked(f[f"attn_b_b{name}"]).reshape(B_GROUPS, P).T
    for name in "vo":
        d[f"w{name}_b"] = f[f"attn_b_w{name}"].T
        d[f"bias_{name}"] = np.broadcast_to(f[f"attn_b_b{name}"], (P, DIM))
    row = np.arange(P)
    copy = row % 32 // B_HEAD
    d["lower_rows"] = np.stack([copy == 1, copy == 2], axis=1).astype(np.float32)
    d["head_rows"] = (row[:, None] // 32 == np.arange(4)).astype(np.float32)
    own, chunk = np.divmod(np.arange(B_HEADS * CHUNKS), CHUNKS)
    c = np.arange(CHUNKS)
    d["mean_select"] = np.broadcast_to((chunk == c[:, None]) / CHUNK, (P, CHUNKS, B_HEADS * CHUNKS)).astype(np.float16)
    d["causal"] = np.broadcast_to(np.where(chunk > c[:, None], -1e30, 0.0).reshape(-1), (P, CHUNKS * B_HEADS * CHUNKS))
    d["causal"] = d["causal"].astype(np.float32)
    d["own_head"] = (own[:, None] == np.arange(DIM) // B_HEAD).astype(np.float32)
    return {k: np.ascontiguousarray(v) for k, v in d.items()}


def kernel(**inputs):
    import concourse.bacc as bacc
    from concourse.bass_utils import run_bass_kernel_spmd

    nc = bacc.Bacc("TRN2", target_bir_lowering=False, num_devices=1)
    arrays = {f"in_{k}": v for k, v in layouts(inputs).items()}
    d = {k[3:]: nc.dram_tensor(k, v.shape, mybir.dt.from_np(v.dtype), kind="ExternalInput").ap()
         for k, v in arrays.items()}
    out = nc.dram_tensor("out_x", (P, TILES, DIM), F32, kind="ExternalOutput").ap()
    program(nc, d, out)
    r = run_bass_kernel_spmd(nc, [arrays], core_ids=[0])
    got = r.results[0]["out_x"]
    return np.ascontiguousarray(got.transpose(1, 0, 2)).reshape(BATCH, SEQ, DIM)
```

```python
from contextlib import ExitStack

import numpy as np

import concourse.bass as bass
from concourse import mybir

F32 = mybir.dt.float32
F16 = mybir.dt.float16
ALU = mybir.AluOpType
ACT = mybir.ActivationFunctionType
AX = mybir.AxisListType

P = 128
BATCH, SEQ, DIM = 8, 512, 128
TOKENS = BATCH * SEQ
TILES = TOKENS // P
BLOCK = 512
TPB = BLOCK // P
BLOCKS = TOKENS // BLOCK
EPS = 1e-5
WSCALE = 64.0

A_HEADS, A_HEAD = 16, 64
A_INNER = A_HEADS * A_HEAD
A_PAIRS = A_HEADS // 2
A_SCALE = float(A_HEAD) ** -0.5
FREQS = 16
Q, QR, K, KR, V = range(5)

B_HEADS, B_HEAD, CHUNK = 16, 8, 128
CHUNKS = SEQ // CHUNK
B_GROUPS = B_HEADS // 4
B_SCALE = float(B_HEAD) ** -0.5

HIDDEN = 512
HT = HIDDEN // P


def at_least(eng, sem, value):
    if not isinstance(value, int) or value > 0:
        eng.wait_ge(sem, value)


class Space:

    def __init__(self, nc, ctx, tag):
        self.nc, self.ctx, self.tag = nc, ctx, tag

    def sb(self, name, shape, dt):
        return self.ctx.enter_context(self.nc.sbuf_tensor(f"{self.tag}_{name}", shape, dt))

    def ps(self, name, shape):
        return self.ctx.enter_context(self.nc.psum_tensor(f"{self.tag}_{name}", shape, F32))

    def sem(self, name):
        return self.ctx.enter_context(self.nc.semaphore(f"{self.tag}_{name}"))


class Norm:

    def __init__(self, s, ident, minus_half, bank):
        self.ident, self.minus_half, self.bank = ident, minus_half, bank
        self.stats = s.sb("stats", [P, TPB, 6], F32)
        self.mean = s.sb("mean", [P, TPB], F32)
        self.apart = s.sb("apart", [P, TPB], F32)
        self.squares = s.sb("squares", [P, TPB], F32)
        self.var_eps = s.sb("var_eps", [P, TPB], F32)
        self.rstd = s.sb("rstd", [P, TPB], F32)
        self.normed = s.sb("normed", [P, TPB, DIM], F32)
        self.stats_ready = s.sem("stats_ready")
        self.moments_ready = s.sem("moments_ready")
        self.moment_steps = s.sem("moment_steps")
        self.rstd_ready = s.sem("rstd_ready")
        self.normed_ready = s.sem("normed_ready")
        self.turned = s.sem("turned")
        self.hi_ready = s.sem("xt_hi_ready")
        self.xt_ready = s.sem("xt_ready")

    def dve_moments(self, dve, n, x4):
        half, st = DIM // 2, self.stats
        for t in range(TPB):
            dve.bn_stats(st[:, t, :], x4[:, t, :]).then_inc(self.stats_ready, 1)
        dve.wait_ge(self.stats_ready, TPB * n + TPB)
        dve.tensor_tensor(self.mean[:], st[:, :, 1], st[:, :, 4], ALU.add).then_inc(self.moment_steps, 1)
        dve.tensor_tensor(self.apart[:], st[:, :, 1], st[:, :, 4], ALU.subtract).then_inc(self.moment_steps, 1)
        dve.tensor_tensor(self.squares[:], st[:, :, 2], st[:, :, 5], ALU.add).then_inc(self.moment_steps, 1)
        dve.wait_ge(self.moment_steps, 6 * n + 3)
        dve.tensor_scalar(self.mean[:], self.mean[:], 0.5, None, ALU.mult).then_inc(self.moment_steps, 1)
        dve.scalar_tensor_tensor(out=self.apart[:], in0=self.apart[:], scalar=half / 2.0, in1=self.apart[:],
                                 op0=ALU.mult, op1=ALU.mult).then_inc(self.moment_steps, 1)
        dve.wait_ge(self.moment_steps, 6 * n + 5)
        dve.tensor_tensor(self.squares[:], self.squares[:], self.apart[:], ALU.add).then_inc(self.moment_steps, 1)
        dve.wait_ge(self.moment_steps, 6 * n + 6)
        dve.tensor_scalar(self.var_eps[:], self.squares[:], 1.0 / DIM, EPS, ALU.mult,
                          ALU.add).then_inc(self.moments_ready, 1)

    def pool_rstd(self, pool, n):
        pool.wait_ge(self.moments_ready, n + 1)
        pool.tensor_tensor(self.rstd[:], self.var_eps[:], self.minus_half[:, 0:TPB],
                           ALU.pow).then_inc(self.rstd_ready, 1)

    def dve_apply(self, dve, n, x4):
        dve.wait_ge(self.rstd_ready, n + 1)
        for t in range(TPB):
            dve.tensor_scalar(self.normed[:, t, :], x4[:, t, :], self.mean[:, t:t + 1], self.rstd[:, t:t + 1],
                              ALU.subtract, ALU.mult).then_inc(self.normed_ready, 1)

    def pe_turn(self, pe, n):
        pe.wait_ge(self.normed_ready, TPB * n + TPB)
        for t in range(TPB):
            last = pe.transpose(self.bank[:, t * P:(t + 1) * P], self.normed[:, t, :], self.ident[:])
        last.then_inc(self.turned, 1)

    def act_hi(self, act, n, hi):
        act.wait_ge(self.turned, n + 1)
        act.activation(hi, self.bank[:], ACT.Copy).then_inc(self.hi_ready, 1)

    def dve_lo(self, dve, n, hi, lo):
        dve.wait_ge(self.hi_ready, n + 1)
        dve.tensor_tensor(lo, self.bank[:], hi, ALU.subtract).then_inc(self.xt_ready, 1)


def three_products(pe, out, stat_hi, stat_lo, mov_hi, mov_lo, first=True, last=True):
    pe.matmul(out, stat_hi, mov_hi, start=first, stop=False)
    pe.matmul(out, stat_hi, mov_lo, start=False, stop=False)
    return pe.matmul(out, stat_lo, mov_hi, start=False, stop=last)


def prepare(nc, d, x_all, ident, minus_half, wa, wf, wb):
    SLICE = 5 * A_INNER // BLOCKS
    with ExitStack() as ctx:
        s = Space(nc, ctx, "p")
        w_raw = s.sb("w_raw", [P, 5 * A_INNER], F32)
        wo_raw = s.sb("wo_raw", [P, A_PAIRS, DIM], F32)
        fourier = s.sb("fourier", [2 * FREQS, SEQ], F32)
        w_four = s.sb("w_four", [2 * FREQS, P], F32)
        b_four = s.sb("b_four", [P, 1], F32)
        b_out = s.sb("b_out", [P, DIM], F32)
        w1_raw = s.sb("w1_raw", [P, HT, DIM], F32)
        w1t_raw = s.sb("w1t_raw", [P, HIDDEN], F32)
        w2t_raw = s.sb("w2t_raw", [P, HT, DIM], F32)
        below = s.sb("below", [P, 2, HIDDEN], F16)
        w2_abs = s.sb("w2_abs", [P, HT, DIM], F32)
        mean_of_rows = s.sb("mean_of_rows", [P, P], F32)
        raw_b = {"k": s.sb("wk_raw", [P, HIDDEN], F32), "q": s.sb("wq_raw", [P, HIDDEN], F32),
                 "v": s.sb("wv_raw", [P, DIM], F32), "o": s.sb("wo_b_raw", [P, DIM], F32)}
        tables_b = ("bias_k", "bias_q", "bias_v", "bias_o", "lower_rows", "head_rows", "mean_select", "causal",
                    "own_head")
        turn_bank = s.ps("turn_bank", [P, BLOCK])
        four_bank = s.ps("four_bank", [P, SEQ])
        alpha_bank = s.ps("alpha_bank", [P, SEQ])
        norm = Norm(s, ident, minus_half, turn_bank)
        x_first_in = s.sem("x_first_in")
        x_rest_in = s.sem("x_rest_in")
        consts_in = s.sem("consts_in")
        tables_in = s.sem("tables_in")
        w_in = s.sem("w_in")
        later_in = s.sem("later_in")
        half_set = s.sem("half_set")
        w_scaled = s.sem("w_scaled")
        w_hi_ready = s.sem("w_hi_ready")
        w_split = s.sem("w_split")
        four_mm = s.sem("four_mm")
        four_k_ready = s.sem("four_k_ready")
        bias_added = s.sem("bias_added")
        other_hi_ready = s.sem("other_hi_ready")
        masks_ready = s.sem("masks_ready")
        alpha_summed = s.sem("alpha_summed")
        alpha1_sum = s.sem("alpha1_sum")
        done = s.sem("done")
        w_hi, w_lo = (wa[k][:].rearrange("p a c -> p (a c)") for k in ("w_hi", "w_lo"))
        to_split = [(wo_raw, wa["wo_hi"], wa["wo_lo"])] + [(t, wb[f"{k}_hi"], wb[f"{k}_lo"]) for k, t in raw_b.items()]
        LATER = 16 * (6 + len(raw_b) + len(tables_b))
        block = ctx.enter_context(nc.Block())

        @block.sync
        def _(sp):
            for to, name in ((ident, "ident"), (b_out, "b_out_a"), (fourier, "fourier"), (w_four, "w_four"),
                             (b_four, "b_four")):
                sp.dma_start(to[:], d[name]).then_inc(consts_in, 16)
            sp.dma_start(w_raw[:], d["w_a"]).then_inc(w_in, 16)
            for half in range(2):
                sp.dma_start(wa["cos"][:, half, :], d["cos"][half]).then_inc(tables_in, 16)
                sp.dma_start(wa["sin"][:, half, :], d["sin"][half]).then_inc(tables_in, 16)
            for to, name in ((wo_raw, "wo_a"), (w1_raw, "w1"), (w1t_raw, "w1t"), (w2t_raw, "w2t"), (wf["b1"], "b1"),
                             (wf["b2"], "b2")):
                sp.dma_start(to[:], d[name]).then_inc(later_in, 16)
            for name, to in raw_b.items():
                sp.dma_start(to[:], d[f"w{name}_b"]).then_inc(later_in, 16)
            for name in tables_b:
                sp.dma_start(wb[name][:], d[name]).then_inc(later_in, 16)
            sp.wait_ge(tables_in, 16 * 4)

        @block.vector
        def _(dve):
            def x_block(n):
                return x_all[:, bass.ds(n * TPB, TPB), :]

            def xt(half, n):
                return wa[half][:, bass.ds(n * BLOCK, BLOCK)]

            dve.memset(minus_half[:], -0.5).then_inc(half_set, 1)
            dve.memset(mean_of_rows[:], 1.0 / HIDDEN).then_inc(masks_ready, 1)
            dve.wait_ge(x_first_in, 16)
            norm.dve_moments(dve, 0, x_all[:, 0:TPB, :])
            dve.wait_ge(x_rest_in, 16)
            with dve.Fori(0, BLOCKS - 1) as n:
                norm.dve_apply(dve, n, x_block(n))
                norm.dve_moments(dve, n + 1, x_block(n + 1))
                norm.dve_lo(dve, n, xt("xt_hi", n), xt("xt_lo", n))
            last = BLOCKS - 1
            norm.dve_apply(dve, last, x_all[:, last * TPB:TILES, :])
            norm.dve_lo(dve, last, wa["xt_hi"][:, last * BLOCK:TOKENS], wa["xt_lo"][:, last * BLOCK:TOKENS])
            dve.wait_ge(four_k_ready, 1)
            dve.tensor_scalar(wa["four"][:, 0, :], wa["four"][:, 1, :], A_SCALE, None, ALU.mult).then_inc(done, 1)
            dve.wait_ge(later_in, LATER)
            dve.scalar_tensor_tensor(out=w2_abs[:], in0=w2t_raw[:], scalar=-1.0, in1=w2t_raw[:], op0=ALU.mult,
                                     op1=ALU.max).then_inc(masks_ready, 1)
            w2_flat = w2t_raw[:].rearrange("p a c -> p (a c)")
            s2_flat = wf["sign2"][:].rearrange("p a c -> p (a c)")
            dve.tensor_scalar(below[:, 0, :], w1t_raw[:], 0.0, None, ALU.is_lt).then_inc(masks_ready, 1)
            dve.tensor_scalar(below[:, 1, :], w2_flat, 0.0, None, ALU.is_lt).then_inc(masks_ready, 1)
            dve.tensor_reduce(wf["alpha1"][:], w1_raw[:], AX.X, ALU.add,
                              apply_absolute_value=True).then_inc(alpha1_sum, 1)
            dve.wait_ge(masks_ready, 4)
            dve.scalar_tensor_tensor(out=wf["sign1"][:], in0=w1t_raw[:], scalar=0.0, in1=below[:, 0, :],
                                     op0=ALU.is_gt, op1=ALU.subtract).then_inc(done, 1)
            dve.scalar_tensor_tensor(out=s2_flat, in0=w2_flat, scalar=0.0, in1=below[:, 1, :],
                                     op0=ALU.is_gt, op1=ALU.subtract).then_inc(done, 1)
            dve.wait_ge(alpha1_sum, 1)
            dve.tensor_scalar(wf["alpha1"][:], wf["alpha1"][:], 1.0 / DIM, None, ALU.mult).then_inc(done, 1)
            dve.tensor_scalar(wb["bias_q"][:], wb["bias_q"][:], B_SCALE, None, ALU.mult).then_inc(done, 1)
            for n, (raw, hi, lo) in enumerate(to_split):
                dve.wait_ge(other_hi_ready, n + 1)
                dve.scalar_tensor_tensor(out=lo[:], in0=raw[:], scalar=WSCALE, in1=hi[:], op0=ALU.mult,
                                         op1=ALU.subtract).then_inc(done, 1)
            dve.wait_ge(alpha_summed, 1)
            dve.tensor_copy(wf["alpha2"][:], alpha_bank[:, 0:DIM]).then_inc(done, 1)

        @block.gpsimd
        def _(pool):
            def add_bias(n):
                pool.wait_ge(norm.normed_ready, TPB * n + TPB)
                x4 = x_all[:, bass.ds(n * TPB, TPB), :]
                pool.tensor_tensor(x4, x4, b_out[:].unsqueeze(1).to_broadcast([P, TPB, DIM]),
                                   ALU.add).then_inc(bias_added, 1)

            def split(n):
                at = bass.ds(n * SLICE, SLICE)
                pool.wait_ge(w_hi_ready, n + 1)
                pool.wait_ge(w_scaled, n + 1)
                pool.tensor_tensor(w_lo[:, at], w_raw[:, at], w_hi[:, at], ALU.subtract).then_inc(w_split, 1)

            pool.wait_ge(half_set, 1)
            pool.wait_ge(consts_in, 16 * 5)
            norm.pool_rstd(pool, 0)
            with pool.Fori(0, BLOCKS - 1) as n:
                add_bias(n)
                norm.pool_rstd(pool, n + 1)
                split(n)
            add_bias(BLOCKS - 1)
            split(BLOCKS - 1)

        @block.scalar
        def _(act):
            act.dma_start(x_all[:, 0:TPB, :], d["x"][:, 0:TPB, :]).then_inc(x_first_in, 16)
            act.dma_start(x_all[:, TPB:TILES, :], d["x"][:, TPB:TILES, :]).then_inc(x_rest_in, 16)
            act.wait_ge(w_in, 16)
            for n in range(BLOCKS):
                at = slice(n * SLICE, (n + 1) * SLICE)
                norm.act_hi(act, n, wa["xt_hi"][:, n * BLOCK:(n + 1) * BLOCK])
                act.activation(w_hi[:, at], w_raw[:, at], ACT.Copy, scale=WSCALE).then_inc(w_hi_ready, 1)
                act.wait_ge(w_hi_ready, n + 1)
                act.activation(w_raw[:, at], w_raw[:, at], ACT.Copy, scale=WSCALE).then_inc(w_scaled, 1)
            act.wait_ge(four_mm, 1)
            act.activation(wa["four"][:, 1, :], four_bank[:], ACT.Identity, bias=b_four[:, 0:1]).then_inc(four_k_ready, 1)
            act.wait_ge(later_in, LATER)
            for raw, hi, _ in to_split:
                act.activation(hi[:], raw[:], ACT.Copy, scale=WSCALE).then_inc(other_hi_ready, 1)

        @block.tensor
        def _(pe):
            pe.wait_ge(consts_in, 16 * 5)
            pe.matmul(four_bank[:], w_four[:], fourier[:], start=True, stop=True).then_inc(four_mm, 1)
            with pe.Fori(0, BLOCKS) as n:
                norm.pe_turn(pe, n)
            pe.wait_ge(masks_ready, 2)
            for j in range(HT):
                mm = pe.matmul(alpha_bank[:, 0:DIM], mean_of_rows[:], w2_abs[:, j, :], start=(j == 0),
                               stop=(j == HT - 1))
            mm.then_inc(alpha_summed, 1)


def attention_a(nc, x_all, ident, wa):
    xt_hi, xt_lo, w_hi, w_lo, wo_hi, wo_lo, cos, sin, four = (
        wa[k] for k in ("xt_hi", "xt_lo", "w_hi", "w_lo", "wo_hi", "wo_lo", "cos", "sin", "four"))
    STEPS = BATCH * A_PAIRS
    HQ = 2
    HEADCOLS = A_HEAD + 1
    Q_COPIES, K_COPIES = 8, 4
    with ExitStack() as ctx:
        s = Space(nc, ctx, "ah")
        cos_part = s.sb("cos_part", [P, 2, SEQ], F32)
        sin_part = s.sb("sin_part", [P, 2, SEQ], F32)
        rot_hi = s.sb("rot_hi", [P, 2, SEQ], F16)
        rot_lo = s.sb("rot_lo", [P, 2, SEQ], F16)
        k_stack = s.sb("k_stack", [P, 2, 2, SEQ], F16)
        qh_stack = s.sb("qh_stack", [P, 2, 2, SEQ], F16)
        ql_stack = s.sb("ql_stack", [P, 2, 2, SEQ], F16)
        v_full = s.sb("v_full", [P, SEQ], F32)
        v_hi = s.sb("v_hi", [P, 2, TPB, 2, HEADCOLS], F16)
        v_lo = s.sb("v_lo", [P, 2, TPB, 2, A_HEAD], F16)
        neg_max = s.sb("neg_max", [P, 2, HQ], F32)
        probs = s.sb("probs", [P, 2, HQ, SEQ], F32)
        pt_hi = s.sb("pt_hi", [P, 2, TPB, HQ * P], F16)
        pt_lo = s.sb("pt_lo", [P, 2, TPB, HQ * P], F16)
        inv_sum = s.sb("inv_sum", [P, 2, HQ], F32)
        heads_out = s.sb("heads_out", [P, 2, TPB, P], F32)
        ot_hi = s.sb("ot_hi", [P, SEQ], F16)
        ot_lo = s.sb("ot_lo", [P, SEQ], F16)
        scores = s.ps("scores", [P, 2, HQ, SEQ])
        pt = s.ps("pt", [P, TPB, HQ * P])
        pv = s.ps("pv", [P, 4, P])
        side = s.ps("side", [P, SEQ])

        scores_ready = s.sem("scores_ready")
        max_ready = s.sem("max_ready")
        exp_ready = s.sem("exp_ready")
        pt_ready = s.sem("pt_ready")
        pt_hi_ready = s.sem("pt_hi_ready")
        pt_split = s.sem("pt_split")
        pv_ready = s.sem("pv_ready")
        inv_ready = s.sem("inv_ready")
        pv_taken = s.sem("pv_taken")
        side_ready = s.sem("side_ready")
        side_taken = s.sem("side_taken")
        side_copied = s.sem("side_copied")
        sin_steps = [s.sem("sin_steps_q"), s.sem("sin_steps_k")]
        rotated = [s.sem("rotated_q"), s.sem("rotated_k")]
        rot_hi_ready = [s.sem("rot_hi_q"), s.sem("rot_hi_k")]
        rot_split = [s.sem("rot_split_q"), s.sem("rot_split_k")]
        stacked = [s.sem("stacked_q"), s.sem("stacked_k")]
        v_copied = s.sem("v_copied")
        v_hi_ready = s.sem("v_hi_ready")
        v_split = s.sem("v_split")
        ot_hi_ready = s.sem("ot_hi_ready")
        ot_split = s.sem("ot_split")
        ones_set = s.sem("ones_set")

        LAST = STEPS - 1

        def side_count(g, slot):
            order = {"q": 0, "qr": 1, "k": 2, "kr": 3, "v": 4, "ot": 5, "op": 6}
            if not isinstance(g, int):
                return 7 * g + 7 + order[slot]
            if g == 0:
                return 9 + {"q": 0, "qr": 1, "k": 2, "kr": 3, "v": 4}[slot]
            if g < LAST - 1:
                return 7 * g + 7 + order[slot]
            base = 7 * (LAST - 1) + 7
            return base + {LAST - 1: {"v": 0, "ot": 1, "op": 2}, LAST: {"ot": 3, "op": 4},
                           STEPS: {"ot": 5, "op": 6}}[g][slot]

        def taken_count(g, slot):
            order = {"q": 0, "qr": 1, "k": 1, "kr": 2, "end": 2}
            if isinstance(g, int) and g == 0:
                return 4 + order[slot]
            if isinstance(g, int) and g >= LAST - 1:
                return 3 * (LAST - 1) + 3 + g - (LAST - 1)
            return 3 * g + 3 + order[slot]

        def run(eng, ahead, step, tail):
            ahead()
            step(0, 0)
            with eng.Fori(0, (STEPS - 4) // 2) as i:
                step(2 * i + 1, 1)
                step(2 * i + 2, 0)
            for g in range(STEPS - 3, STEPS):
                step(g, g % 2)
            tail()

        def is_last(g, steps=1):
            return isinstance(g, int) and g >= STEPS - steps

        def is_first(g):
            return isinstance(g, int) and g == 0

        def unit_after(g, u, ahead):
            return g + (u + ahead) // 4, (u + ahead) % 4

        def rotate(eng, which, n, cos_count):
            eng.wait_ge(side_copied, 2 * n + which + 1)
            eng.tensor_tensor(sin_part[:, which, :], sin_part[:, which, :], sin[:, which, :],
                               ALU.mult).then_inc(sin_steps[which], 1)
            eng.wait_ge(sin_steps[which], 2 * n + 1)
            eng.tensor_tensor(sin_part[:, which, :], sin_part[:, which, :], four[:, which, :],
                               ALU.add).then_inc(sin_steps[which], 1)
            eng.wait_ge(sin_steps[which], 2 * n + 2)
            eng.wait_ge(side_taken, cos_count)
            eng.tensor_tensor(cos_part[:, which, :], cos_part[:, which, :], sin_part[:, which, :],
                               ALU.add).then_inc(rotated[which], 1)

        def rotated_lo(eng, which, n):
            eng.wait_ge(rot_hi_ready[which], n + 1)
            eng.tensor_tensor(rot_lo[:, which, :], cos_part[:, which, :], rot_hi[:, which, :],
                               ALU.subtract).then_inc(rot_split[which], 1)

        block = ctx.enter_context(nc.Block())

        @block.sync
        def _(sp):
            def stack(n, par):
                for which in (0, 1):
                    sp.wait_ge(rot_split[which], n + 1)
                    if not isinstance(n, int) or n > 1:
                        sp.wait_ge(scores_ready, 4 * n - 4)
                    for h in range(2):
                        own = slice(h * A_HEAD, (h + 1) * A_HEAD)
                        for half in range(2):
                            to = slice(half * A_HEAD, (half + 1) * A_HEAD)
                            if which == 0:
                                sp.dma_start(qh_stack[to, par, h, :], rot_hi[own, 0, :]).then_inc(stacked[0], 16)
                                sp.dma_start(ql_stack[to, par, h, :], rot_lo[own, 0, :]).then_inc(stacked[0], 16)
                            else:
                                part = rot_lo if half else rot_hi
                                sp.dma_start(k_stack[to, par, h, :], part[own, 1, :]).then_inc(stacked[1], 16)

            def ahead():
                stack(0, 0)
                stack(1, 1)

            def step(g, par):
                if not is_last(g, 2):
                    stack(g + 2, par)

            run(sp, ahead, step, lambda: None)
            sp.wait_ge(stacked[0], 16 * Q_COPIES * STEPS)
            sp.wait_ge(stacked[1], 16 * K_COPIES * STEPS)

        @block.tensor
        def _(pe):
            def project(kind, n):
                w = bass.ds(n % A_PAIRS * P, P)
                x = bass.ds(n // A_PAIRS * SEQ, SEQ)
                three_products(pe, side[:], w_hi[:, kind, w], w_lo[:, kind, w], xt_hi[:, x],
                               xt_lo[:, x]).then_inc(side_ready, 1)

            def project_v(n):
                w = bass.ds(n % A_PAIRS * P, P)
                for t in range(TPB):
                    x = bass.ds(n // A_PAIRS * SEQ + t * P, P)
                    done = three_products(pe, side[:, t * P:(t + 1) * P], xt_hi[:, x], xt_lo[:, x],
                                          w_hi[:, V, w], w_lo[:, V, w])
                done.then_inc(side_ready, 1)

            def score(g, par, u):
                h, half = u // 2, u % 2
                if u == 0:
                    pe.wait_ge(stacked[0], 16 * Q_COPIES * (g + 1))
                    pe.wait_ge(stacked[1], 16 * K_COPIES * (g + 1))
                at_least(pe, exp_ready, HQ * (4 * g + u - 1))
                for t in range(HQ):
                    q = slice((half * HQ + t) * P, (half * HQ + t + 1) * P)
                    pe.matmul(scores[:, u % 2, t, :], qh_stack[:, par, h, q], k_stack[:, par, h, :],
                              start=True, stop=False)
                    done = pe.matmul(scores[:, u % 2, t, :], ql_stack[:, par, h, q], k_stack[:, par, h, :],
                                     start=False, stop=True)
                done.then_inc(scores_ready, 1)

            def turn(g, u):
                at_least(pe, pt_split, 4 * g + u)
                for t in range(HQ):
                    pe.wait_ge(exp_ready, HQ * (4 * g + u) + t + 1)
                    for j in range(TPB):
                        done = pe.transpose(pt[:, j, t * P:(t + 1) * P], probs[:, u % 2, t, j * P:(j + 1) * P],
                                            ident[:])
                done.then_inc(pt_ready, 1)

            def values(g, par, u):
                h = u // 2
                if u == 0:
                    pe.wait_ge(v_split, g + 1)
                pe.wait_ge(pt_split, 4 * g + u + 1)
                at_least(pe, pv_taken, 4 * g + u)
                for t in range(HQ):
                    for j in range(TPB):
                        p_hi = pt_hi[:, u % 2, j, t * P:(t + 1) * P]
                        p_lo = pt_lo[:, u % 2, j, t * P:(t + 1) * P]
                        pe.matmul(pv[:, t, 0:HEADCOLS], p_hi, v_hi[:, par, j, h, :], start=(j == 0), stop=False)
                        pe.matmul(pv[:, t, 0:A_HEAD], p_hi, v_lo[:, par, j, h, :], start=False, stop=False)
                        done = pe.matmul(pv[:, t, 0:HEADCOLS], p_lo, v_hi[:, par, j, h, :], start=False,
                                         stop=(j == TPB - 1))
                done.then_inc(pv_ready, 1)

            def turn_out(p, par):
                pe.wait_ge(pv_taken, 4 * p + 4)
                for t in range(TPB):
                    done = pe.transpose(side[:, t * P:(t + 1) * P], heads_out[:, par, t, :], ident[:])
                done.then_inc(side_ready, 1)

            def project_out(p):
                pe.wait_ge(ot_split, p + 1)
                pair = bass.ds(p % A_PAIRS, 1)
                o_hi = wo_hi[:, pair, :].rearrange("p a c -> p (a c)")
                o_lo = wo_lo[:, pair, :].rearrange("p a c -> p (a c)")
                for t in range(TPB):
                    tok = slice(t * P, (t + 1) * P)
                    done = three_products(pe, side[:, tok], ot_hi[:, tok], ot_lo[:, tok], o_hi, o_lo)
                done.then_inc(side_ready, 1)

            def after_score(g, par, u):
                g2, u2 = unit_after(g, u, 2)
                if not (is_last(g) and u >= 2):
                    score(g2, par if u < 2 else 1 - par, u2)

            def before_values(g, par, u):
                if u > 0:
                    values(g, par, u - 1)
                elif not is_first(g):
                    values(g - 1, 1 - par, 3)

            def step(g, par):
                for u, (cos_kind, sin_kind, cos_slot, sin_slot) in enumerate(((Q, QR, "q", "qr"), (K, KR, "k", "kr"))):
                    turn(g, u)
                    if not is_last(g, 2):
                        if is_first(g):
                            pe.wait_ge(v_copied, 1)
                        elif u == 0:
                            pe.wait_ge(v_copied, g + 1)
                            pe.wait_ge(side_taken, taken_count(g, "q"))
                        if u == 1:
                            pe.wait_ge(side_copied, 2 * g + 5)
                        project(cos_kind, g + 2)
                    after_score(g, par, u)
                    if not is_last(g, 2):
                        pe.wait_ge(side_taken, taken_count(g, sin_slot))
                        project(sin_kind, g + 2)
                    before_values(g, par, u)
                turn(g, 2)
                if not is_last(g):
                    if is_last(g, 2):
                        pe.wait_ge(side_taken, taken_count(g, "end"))
                    else:
                        pe.wait_ge(side_copied, 2 * g + 6)
                    project_v(g + 1)
                after_score(g, par, 2)
                before_values(g, par, 2)
                if not is_first(g):
                    if is_last(g):
                        pe.wait_ge(side_taken, taken_count(g, "end"))
                    else:
                        pe.wait_ge(v_copied, g + 2)
                    turn_out(g - 1, 1 - par)
                turn(g, 3)
                after_score(g, par, 3)
                if not is_first(g):
                    project_out(g - 1)
                before_values(g, par, 3)

            def ahead():
                for n in (0, 1):
                    for which, (cos_kind, sin_kind) in enumerate(((Q, QR), (K, KR))):
                        at_least(pe, side_copied, 2 * n + which)
                        project(cos_kind, n)
                        pe.wait_ge(side_taken, 2 * n + which + 1)
                        project(sin_kind, n)
                pe.wait_ge(side_copied, 4)
                project_v(0)
                score(0, 0, 0)
                score(0, 0, 1)

            def tail():
                values(LAST, LAST % 2, 3)
                pe.wait_ge(side_taken, taken_count(STEPS, "end"))
                turn_out(LAST, LAST % 2)
                project_out(LAST)

            run(pe, ahead, step, tail)

        @block.scalar
        def _(act):
            def exps(g, u):
                act.wait_ge(max_ready, 4 * g + u + 1)
                at_least(act, pt_ready, 4 * g + u - 1)
                for t in range(HQ):
                    act.activation(probs[:, u % 2, t, :], scores[:, u % 2, t, :], ACT.Exp,
                                   bias=neg_max[:, u % 2, t:t + 1]).then_inc(exp_ready, 1)

            def probs_hi(g, u):
                act.wait_ge(pt_ready, 4 * g + u + 1)
                at_least(act, pv_ready, 4 * g + u - 1)
                act.activation(pt_hi[:, u % 2, :, :], pt[:], ACT.Copy).then_inc(pt_hi_ready, 1)

            def copy_rotated(which, n, count):
                act.wait_ge(side_ready, count + 1)
                at_least(act, rot_split[which], n)
                act.activation(sin_part[:, which, :], side[:], ACT.Copy).then_inc(side_copied, 1)

            def rotated_hi(which, n):
                act.wait_ge(rotated[which], n + 1)
                at_least(act, stacked[which], 16 * (Q_COPIES, K_COPIES)[which] * n)
                act.activation(rot_hi[:, which, :], cos_part[:, which, :], ACT.Copy).then_inc(rot_hi_ready[which], 1)

            def value_full(n, count):
                act.wait_ge(side_ready, count + 1)
                at_least(act, v_split, n)
                act.activation(v_full[:], side[:], ACT.Copy, scale=1.0 / WSCALE).then_inc(v_copied, 1)

            def value_hi(n, par):
                act.wait_ge(v_copied, n + 1)
                at_least(act, pv_ready, 4 * n - 4)
                act.activation(v_hi[:, par, :, :, 0:A_HEAD], v_full[:].rearrange("p (t h c) -> p t h c", t=TPB, h=2),
                               ACT.Copy).then_inc(v_hi_ready, 1)

            def out_hi(p, count):
                act.wait_ge(side_ready, count + 1)
                act.activation(ot_hi[:], side[:], ACT.Copy).then_inc(ot_hi_ready, 1)

            def next_exps(g, u):
                if not (is_last(g) and u == 3):
                    exps(*unit_after(g, u, 1))

            def step(g, par):
                for u in range(4):
                    if u == 3 and not is_first(g):
                        out_hi(g - 1, side_count(g, "ot"))
                    probs_hi(g, u)
                    if u == 2 and not is_last(g):
                        value_full(g + 1, side_count(g, "v"))
                    next_exps(g, u)
                    if u == 3 and not is_last(g):
                        value_hi(g + 1, 1 - par)
                    if u < 2 and not is_last(g, 2):
                        copy_rotated(u, g + 2, side_count(g, ("qr", "kr")[u]))
                    if u >= 2 and not is_last(g, 2):
                        rotated_hi(u - 2, g + 2)

            def ahead():
                act.wait_ge(ones_set, 1)
                for n in (0, 1):
                    for which in (0, 1):
                        copy_rotated(which, n, 4 * n + 2 * which + 1)
                    for which in (0, 1):
                        rotated_hi(which, n)
                value_full(0, 8)
                value_hi(0, 0)
                exps(0, 0)

            run(act, ahead, step, lambda: out_hi(LAST, side_count(STEPS, "ot")))

        @block.gpsimd
        def _(pool):
            def value_lo(n, par):
                pool.wait_ge(v_hi_ready, n + 1)
                pool.tensor_tensor(v_lo[:, par, :, :, :].rearrange("p t h c -> p (t h) c"),
                                   v_full[:].rearrange("p (a c) -> p a c", c=A_HEAD),
                                   v_hi[:, par, :, :, 0:A_HEAD].rearrange("p t h c -> p (t h) c"),
                                   ALU.subtract).then_inc(v_split, 1)

            def step(g, par):
                if not is_last(g, 2):
                    rotate(pool, 0, g + 2, taken_count(g, "q") + 1)
                    rotate(pool, 1, g + 2, taken_count(g, "k") + 1)
                    rotated_lo(pool, 0, g + 2)
                    rotated_lo(pool, 1, g + 2)
                if not is_last(g):
                    value_lo(g + 1, 1 - par)

            def ahead():
                for n in (0, 1):
                    rotate(pool, 0, n, 2 * n + 1)
                    rotated_lo(pool, 0, n)
                value_lo(0, 0)

            run(pool, ahead, step, lambda: None)

        @block.vector
        def _(dve):
            def maxima(g, u):
                dve.wait_ge(scores_ready, 4 * g + u + 1)
                at_least(dve, exp_ready, HQ * (4 * g + u - 1))
                dve.tensor_reduce(neg_max[:, u % 2, :], scores[:, u % 2, :, :], AX.X, ALU.max,
                                  negate=True).then_inc(max_ready, 1)

            def probs_lo(g, u):
                dve.wait_ge(pt_hi_ready, 4 * g + u + 1)
                dve.tensor_tensor(pt_lo[:, u % 2, :, :], pt[:], pt_hi[:, u % 2, :, :],
                                  ALU.subtract).then_inc(pt_split, 1)

            def normalise(g, par, u):
                h, half = u // 2, u % 2
                dve.wait_ge(pv_ready, 4 * g + u + 1)
                dve.reciprocal(inv_sum[:, u % 2, :], pv[:, 0:HQ, A_HEAD]).then_inc(inv_ready, 1)
                dve.wait_ge(inv_ready, 4 * g + u + 1)
                dve.tensor_tensor(heads_out[:, par, half * HQ:(half + 1) * HQ, h * A_HEAD:(h + 1) * A_HEAD],
                                  pv[:, 0:HQ, 0:A_HEAD],
                                  inv_sum[:, u % 2, :].unsqueeze(2).to_broadcast([P, HQ, A_HEAD]),
                                  ALU.mult).then_inc(pv_taken, 1)

            def times_cos(which, n, count):
                dve.wait_ge(side_ready, count + 1)
                at_least(dve, rot_split[which], n)
                dve.tensor_tensor(cos_part[:, which, :], side[:], cos[:, which, :], ALU.mult).then_inc(side_taken, 1)

            def out_lo(p):
                dve.wait_ge(ot_hi_ready, p + 1)
                dve.tensor_tensor(ot_lo[:], side[:], ot_hi[:], ALU.subtract).then_inc(ot_split, 1)

            def add_out(p, count, before):
                dve.wait_ge(side_ready, count + 1)
                dve.wait_ge(side_taken, before)
                x4 = x_all[:, bass.ds(p // A_PAIRS * TPB, TPB), :].rearrange("p t c -> p (t c)")
                dve.scalar_tensor_tensor(out=x4, in0=side[:], scalar=1.0 / WSCALE, in1=x4, op0=ALU.mult,
                                         op1=ALU.add).then_inc(side_taken, 1)

            def before_normalise(g, par, u):
                if u > 0:
                    normalise(g, par, u - 1)
                elif not is_first(g):
                    normalise(g - 1, 1 - par, 3)

            def after_maxima(g, u):
                if not (is_last(g) and u >= 2):
                    maxima(*unit_after(g, u, 2))

            def step(g, par):
                for which, slot in enumerate(("q", "k")):
                    if not is_last(g, 2):
                        times_cos(which, g + 2, side_count(g, slot))
                    probs_lo(g, which)
                    after_maxima(g, which)
                    before_normalise(g, par, which)
                probs_lo(g, 2)
                after_maxima(g, 2)
                before_normalise(g, par, 2)
                if not is_first(g):
                    out_lo(g - 1)
                probs_lo(g, 3)
                if not is_first(g):
                    add_out(g - 1, side_count(g, "op"), taken_count(g, "end"))
                after_maxima(g, 3)
                before_normalise(g, par, 3)

            def ahead():
                dve.memset(v_hi[:], 1.0).then_inc(ones_set, 1)
                for n in (0, 1):
                    for which in (0, 1):
                        times_cos(which, n, 4 * n + 2 * which)
                    rotate(dve, 1, n, 2 * n + 2)
                    rotated_lo(dve, 1, n)
                maxima(0, 0)
                maxima(0, 1)

            def tail():
                normalise(LAST, LAST % 2, 3)
                out_lo(LAST)
                add_out(LAST, side_count(STEPS, "op"), taken_count(STEPS, "end"))

            run(dve, ahead, step, tail)


def feed_forward(nc, x_all, ident, minus_half, w, tag, out=None):
    with ExitStack() as ctx:
        s = Space(nc, ctx, tag)
        xt_hi = s.sb("xt_hi", [P, 2, BLOCK], F16)
        xt_lo = s.sb("xt_lo", [P, 2, BLOCK], F16)
        hidden = s.sb("hidden", [P, 2, HT, BLOCK], F32)
        hidden_hi = s.sb("hidden_hi", [P, 2, HT, BLOCK], F16)
        hidden_lo = s.sb("hidden_lo", [P, 2, HT, BLOCK], F16)
        scaled = s.sb("scaled", [P, TPB, DIM], F32)
        turn_bank = s.ps("turn_bank", [P, BLOCK])
        up = s.ps("up", [P, HT, BLOCK])
        down = s.ps("down", [P, TPB, DIM])
        norm = Norm(s, ident, minus_half, turn_bank)
        up_ready = s.sem("up_ready")
        gelu_ready = s.sem("gelu_ready")
        hi_by_scalar = s.sem("hi_by_scalar")
        hi_by_vector = s.sem("hi_by_vector")
        hidden_split = s.sem("hidden_split")
        down_ready = s.sem("down_ready")
        down_free = s.sem("down_free")
        scaled_ready = s.sem("scaled_ready")
        summed = s.sem("summed")

        def x_block(n):
            if isinstance(n, int):
                return x_all[:, n * TPB:(n + 1) * TPB, :]
            return x_all[:, bass.ds(n * TPB, TPB), :]

        def steps(eng, step):
            with eng.Fori(0, BLOCKS // 2 - 2) as i:
                step(2 * i, 0)
                step(2 * i + 1, 1)
            for n in range(BLOCKS - 4, BLOCKS):
                step(n, n % 2)

        def has(n):
            return not isinstance(n, int) or n < BLOCKS

        stored = s.sem("stored")
        block = ctx.enter_context(nc.Block())

        if out is not None:
            @block.sync
            def _(sp):
                with sp.Fori(0, BLOCKS) as n:
                    at = bass.ds(n * TPB, TPB)
                    sp.wait_ge(summed, n + 2)
                    sp.dma_start(out[:, at, :], x_all[:, at, :]).then_inc(stored, 16)
                sp.wait_ge(stored, 16 * BLOCKS)

        @block.tensor
        def _(pe):
            def expand(n, par):
                pe.wait_ge(norm.xt_ready, n + 1)
                for j in range(HT):
                    if not (isinstance(n, int) and n == 0):
                        pe.wait_ge(gelu_ready, HT * n - HT + j + 1)
                    hid = slice(j * P, (j + 1) * P)
                    pe.matmul(up[:, j, :], w["sign1"][:, hid], xt_hi[:, par, :], start=True, stop=False)
                    pe.matmul(up[:, j, :], w["sign1"][:, hid], xt_lo[:, par, :], start=False,
                              stop=True).then_inc(up_ready, 1)

            def contract(n, par):
                pe.wait_ge(hidden_split, HT * n + HT)
                pe.wait_ge(down_free, n + 1)
                for t in range(TPB):
                    tok = slice(t * P, (t + 1) * P)
                    for j in range(HT):
                        pe.matmul(down[:, t, :], hidden_hi[:, par, j, tok], w["sign2"][:, j, :], start=(j == 0),
                                  stop=False)
                        mm = pe.matmul(down[:, t, :], hidden_lo[:, par, j, tok], w["sign2"][:, j, :], start=False,
                                       stop=(j == HT - 1))
                mm.then_inc(down_ready, 1)

            def step(n, par):
                if has(n + 1):
                    expand(n + 1, 1 - par)
                if has(n + 2):
                    norm.pe_turn(pe, n + 2)
                contract(n, par)

            pe.sem_inc(down_ready, 1)
            norm.pe_turn(pe, 0)
            expand(0, 0)
            norm.pe_turn(pe, 1)
            steps(pe, step)

        @block.scalar
        def _(act):
            def gelu(n, par, j):
                act.wait_ge(up_ready, HT * n + j + 1)
                act.activation(hidden[:, par, j, :], up[:, j, :], ACT.Gelu, bias=w["b1"][:, j:j + 1],
                               scale=w["alpha1"][:, j:j + 1]).then_inc(gelu_ready, 1)

            def upper(n, par, j):
                act.wait_ge(gelu_ready, HT * n + j + 1)
                act.activation(hidden_hi[:, par, j, :], hidden[:, par, j, :], ACT.Copy).then_inc(hi_by_scalar, 1)

            def activate(n, par):
                at_least(act, down_ready, n)
                gelu(n, par, 0)
                gelu(n, par, 1)
                upper(n, par, 0)
                gelu(n, par, 2)
                upper(n, par, 1)
                gelu(n, par, 3)

            def step(n, par):
                if has(n + 1):
                    activate(n + 1, 1 - par)
                if has(n + 2):
                    norm.act_hi(act, n + 2, xt_hi[:, par, :])

            norm.act_hi(act, 0, xt_hi[:, 0, :])
            norm.act_hi(act, 1, xt_hi[:, 1, :])
            activate(0, 0)
            steps(act, step)

        @block.gpsimd
        def _(pool):
            def split(n, par):
                for j in range(HT):
                    if j < 2:
                        pool.wait_ge(hi_by_scalar, 2 * n + j + 1)
                    else:
                        pool.wait_ge(hi_by_vector, 2 * n + j - 1)
                    pool.tensor_tensor(hidden_lo[:, par, j, :], hidden[:, par, j, :], hidden_hi[:, par, j, :],
                                       ALU.subtract).then_inc(hidden_split, 1)

            def step(n, par):
                if has(n + 1):
                    split(n + 1, 1 - par)
                if has(n + 4):
                    norm.pool_rstd(pool, n + 4)

            for n in range(4):
                norm.pool_rstd(pool, n)
            split(0, 0)
            steps(pool, step)

        @block.vector
        def _(dve):
            def combine(n):
                x4 = x_block(n)
                dve.wait_ge(summed, n + 1)
                dve.tensor_tensor(x4, x4, w["b2"][:].unsqueeze(1).to_broadcast([P, TPB, DIM]),
                                  ALU.add).then_inc(scaled_ready, 1)
                dve.wait_ge(down_ready, n + 2)
                dve.tensor_tensor(scaled[:], down[:], w["alpha2"][:].unsqueeze(1).to_broadcast([P, TPB, DIM]),
                                  ALU.mult).then_inc(down_free, 1)
                dve.wait_ge(down_free, n + 2)
                dve.wait_ge(scaled_ready, n + 1)
                dve.tensor_tensor(x4, x4, scaled[:], ALU.add).then_inc(summed, 1)

            def upper(n, par):
                for j in (2, 3):
                    dve.wait_ge(gelu_ready, HT * n + j + 1)
                    dve.tensor_copy(hidden_hi[:, par, j, :], hidden[:, par, j, :]).then_inc(hi_by_vector, 1)

            def lower(n, par):
                norm.dve_lo(dve, n, xt_hi[:, par, :], xt_lo[:, par, :])

            def step(n, par):
                if has(n + 1):
                    upper(n + 1, 1 - par)
                if has(n + 2):
                    lower(n + 2, par)
                if has(n + 3):
                    norm.dve_apply(dve, n + 3, x_block(n + 3))
                if has(n + 4):
                    norm.dve_moments(dve, n + 4, x_block(n + 4))
                combine(n)

            dve.sem_inc(down_free, 1)
            dve.sem_inc(summed, 1)
            norm.dve_moments(dve, 0, x_block(0))
            for n in range(3):
                norm.dve_apply(dve, n, x_block(n))
                norm.dve_moments(dve, n + 1, x_block(n + 1))
                if n < 2:
                    lower(n, n)
            upper(0, 0)
            steps(dve, step)


def attention_b(nc, x_all, ident, minus_half, w):
    SEQS = BATCH
    UNITS = 2 * CHUNKS
    UH = B_HEADS // 2
    VC = B_HEAD + 1
    INTER = B_HEADS * CHUNKS
    SIDE = ("xt", "k0", "k1", "k2", "k3", "q0", "q1", "q2", "q3", "v", "at", "si", "io", "ot", "op")
    ACT_TAKES = ("k0", "k1", "k2", "k3", "q0", "q1", "q2", "q3", "io")
    OWN = ("at", "io")
    OUTPUT = ("ot", "op")
    with ExitStack() as ctx:
        s = Space(nc, ctx, "b")
        xt_hi = s.sb("xt_hi", [P, SEQ], F16)
        xt_lo = s.sb("xt_lo", [P, SEQ], F16)
        xm = s.sb("xm", [P, CHUNKS], F32)
        xm_hi = s.sb("xm_hi", [P, CHUNKS], F16)
        xm_lo = s.sb("xm_lo", [P, CHUNKS], F16)
        full = s.sb("full", [P, B_GROUPS, SEQ], F32)
        lower = s.sb("lower", [P, B_GROUPS, SEQ], F16)
        q_stack = s.sb("q_stack", [P, 2, B_GROUPS, SEQ], F16)
        k_stack = s.sb("k_stack", [P, B_GROUPS, SEQ], F16)
        k_heads = s.sb("k_heads", [P, 2, B_GROUPS, 4, SEQ], F16)
        km_full = s.sb("km_full", [P, B_GROUPS, CHUNKS], F32)
        km_lower = s.sb("km_lower", [P, B_GROUPS, CHUNKS], F16)
        km_stack = s.sb("km_stack", [P, B_GROUPS, CHUNKS], F16)
        km_heads = s.sb("km_heads", [P, B_GROUPS, 4, CHUNKS], F16)
        v_full = s.sb("v_full", [P, CHUNKS, DIM], F32)
        v_hi = s.sb("v_hi", [P, 2, CHUNKS, B_HEADS, VC], F16)
        v_lo = s.sb("v_lo", [P, 2, CHUNKS, B_HEADS, B_HEAD], F16)
        vm_full = s.sb("vm_full", [INTER, DIM], F32)
        vm_hi = s.sb("vm_hi", [INTER, DIM], F16)
        vm_lo = s.sb("vm_lo", [INTER, DIM], F16)
        inter = s.sb("inter", [P, CHUNKS * INTER], F32)
        inter_max = s.sb("inter_max", [P, INTER], F32)
        inter_exp = s.sb("inter_exp", [P, CHUNKS * INTER], F32)
        inter_sum = s.sb("inter_sum", [P, INTER], F32)
        inter_inv = s.sb("inter_inv", [P, INTER], F32)
        inter_probs = s.sb("inter_probs", [P, CHUNKS + 1, INTER], F32)
        at_hi = s.sb("at_hi", [INTER, SEQ], F16)
        at_lo = s.sb("at_lo", [INTER, SEQ], F16)
        inter_out = s.sb("inter_out", [P, 2, CHUNKS, DIM], F32)
        neg_max = s.sb("neg_max", [P, 2, UH], F32)
        probs = s.sb("probs", [P, 2, UH, CHUNK], F32)
        pt_hi = s.sb("pt_hi", [P, 2, UH, CHUNK], F16)
        pt_lo = s.sb("pt_lo", [P, 2, UH, CHUNK], F16)
        inv_sum = s.sb("inv_sum", [P, UH], F32)
        heads_out = s.sb("heads_out", [P, 2, CHUNKS, DIM], F32)
        ot_hi = s.sb("ot_hi", [P, SEQ], F16)
        ot_lo = s.sb("ot_lo", [P, SEQ], F16)
        scores = s.ps("scores", [P, 2, UH, CHUNK])
        pt = s.ps("pt", [P, UH, CHUNK])
        small = s.ps("small", [P, SEQ])
        pv = small[:, 0:UH * VC].rearrange("p (h e) -> p h e", h=UH)
        k_means = small[:, 128:128 + B_GROUPS * CHUNKS]
        v_means = small[0:INTER, 256:256 + DIM]
        side = s.ps("side", [P, SEQ])
        norm = Norm(s, ident, minus_half, side)
        means_ready = s.sem("means_ready")
        means_taken = s.sem("means_taken")
        side_ready = s.sem("side_ready")
        dve_took = s.sem("dve_took")
        act_took = s.sem("act_took")
        scores_ready = s.sem("scores_ready")
        max_ready = s.sem("max_ready")
        exp_ready = s.sem("exp_ready")
        pt_ready = s.sem("pt_ready")
        pt_hi_ready = s.sem("pt_hi_ready")
        pt_split = s.sem("pt_split")
        pv_ready = s.sem("pv_ready")
        inv_ready = s.sem("inv_ready")
        intra_ready = s.sem("intra_ready")
        out_ready = s.sem("out_ready")
        xm_split = s.sem("xm_split")
        k_lower_ready = s.sem("k_lower_ready")
        q_lower_ready = s.sem("q_lower_ready")
        stack_ready = s.sem("stack_ready")
        k_heads_ready = s.sem("k_heads_ready")
        km_steps = s.sem("km_steps")
        v_hi_ready = s.sem("v_hi_ready")
        v_split = s.sem("v_split")
        vm_steps = s.sem("vm_steps")
        inter_steps = s.sem("inter_steps")
        inter_exp_ready = s.sem("inter_exp_ready")
        at_hi_ready = s.sem("at_hi_ready")
        ot_hi_ready = s.sem("ot_hi_ready")
        bias_added = s.sem("bias_added")
        ones_set = s.sem("ones_set")

        def uses(n, item):
            def kinds(items):
                by_act = sum(i in ACT_TAKES for i in items)
                return len(items), len(items) - by_act, by_act

            ahead = [i for i in SIDE if i not in OUTPUT + OWN]
            first = [i for i in SIDE if i not in OUTPUT]
            t = n + (2 if item in OUTPUT else 1 if item in OWN else 0)
            if not isinstance(t, int):
                start, per = kinds(ahead + first + list(SIDE[:SIDE.index(item)])), kinds(SIDE)
                return tuple(p * (t - 2) + x for p, x in zip(per, start))
            parts = [ahead, first] + [list(SIDE)] * (SEQS - 2) + [[*OWN, *OUTPUT], list(OUTPUT)]
            return kinds([i for part in parts[:t] for i in part] + parts[t][:parts[t].index(item)])

        def all_of(n_or_b, item):
            return uses(n_or_b, item)[0]

        def is_last(b):
            return isinstance(b, int) and b == SEQS - 1

        def is_first(b):
            return isinstance(b, int) and b == 0

        def run(eng, ahead, step, tail):
            ahead()
            step(0, 0)
            with eng.Fori(0, (SEQS - 4) // 2) as i:
                step(2 * i + 1, 1)
                step(2 * i + 2, 0)
            for b in range(SEQS - 3, SEQS):
                step(b, b % 2)
            tail()

        def unit_after(b, u, ahead):
            return b + (u + ahead) // UNITS, (u + ahead) % UNITS

        def x_block(n):
            if isinstance(n, int):
                return x_all[:, n * TPB:(n + 1) * TPB, :]
            return x_all[:, bass.ds(n * TPB, TPB), :]

        block = ctx.enter_context(nc.Block())

        @block.tensor
        def _(pe):
            def bank_free(n, item):
                _, by_dve, by_act = uses(n, item)
                at_least(pe, dve_took, by_dve)
                at_least(pe, act_took, by_act)

            def turn_x(n):
                bank_free(n, "xt")
                pe.wait_ge(norm.normed_ready, TPB * n + TPB)
                for t in range(TPB):
                    mm = pe.transpose(side[:, t * P:(t + 1) * P], norm.normed[:, t, :], ident[:])
                mm.then_inc(side_ready, 1)

            def project(name, g, n):
                bank_free(n, f"{name}{g}")
                rows = slice(g * P, (g + 1) * P)
                three_products(pe, side[:], w[f"{name}_hi"][:, rows], w[f"{name}_lo"][:, rows], xt_hi[:],
                               xt_lo[:]).then_inc(side_ready, 1)

            def key_means(n):
                at_least(pe, intra_ready, UNITS * (n - 1) + 3)
                pe.wait_ge(xm_split, 2 * n + 2)
                for g in range(B_GROUPS):
                    rows = slice(g * P, (g + 1) * P)
                    mm = three_products(pe, k_means[:, g * CHUNKS:(g + 1) * CHUNKS], w["k_hi"][:, rows],
                                        w["k_lo"][:, rows], xm_hi[:], xm_lo[:])
                mm.then_inc(means_ready, 1)

            def project_v(n):
                bank_free(n, "v")
                for c in range(CHUNKS):
                    tok = slice(c * P, (c + 1) * P)
                    mm = three_products(pe, side[:, tok], xt_hi[:, tok], xt_lo[:, tok], w["v_hi"][:], w["v_lo"][:])
                mm.then_inc(side_ready, 1)

            def inter_scores(n, par):
                bank_free(n, "si")
                pe.wait_ge(stack_ready, 8 * n + 8)
                pe.wait_ge(km_steps, 6 * n + 6)
                for c in range(CHUNKS):
                    for g in range(B_GROUPS):
                        at = (c * B_GROUPS + g) * 16
                        mm = pe.matmul(side[:, at:at + 16], q_stack[:, par, g, c * P:(c + 1) * P],
                                       km_heads[:, g, :, :], start=True, stop=True)
                mm.then_inc(side_ready, 1)

            def value_means(n, par):
                at_least(pe, intra_ready, UNITS * (n - 1) + 6)
                pe.wait_ge(means_taken, 2 * n + 1)
                pe.wait_ge(v_split, n + 1)
                for c in range(CHUNKS):
                    pe.matmul(v_means, w["mean_select"][:, c, :], v_hi[:, par, c, :, 0:B_HEAD],
                              start=(c == 0), stop=False)
                    mm = pe.matmul(v_means, w["mean_select"][:, c, :], v_lo[:, par, c, :, :],
                                   start=False, stop=(c == CHUNKS - 1))
                mm.then_inc(means_ready, 1)

            def turn_inter(n):
                bank_free(n, "at")
                pe.wait_ge(ones_set, 2)
                pe.wait_ge(inter_steps, 5 * n + 5)
                for c in range(CHUNKS):
                    mm = pe.transpose(side[:, c * P:(c + 1) * P],
                                      inter_probs[:, c:c + 2, :].rearrange("p c i -> p (c i)"), ident[:])
                mm.then_inc(side_ready, 1)

            def inter_product(n):
                bank_free(n, "io")
                pe.wait_ge(vm_steps, 2 * n + 2)
                for c in range(CHUNKS):
                    tok = slice(c * P, (c + 1) * P)
                    mm = three_products(pe, side[:, tok], at_hi[:, tok], at_lo[:, tok], vm_hi[:], vm_lo[:])
                mm.then_inc(side_ready, 1)

            def turn_out(p, par):
                bank_free(p, "ot")
                pe.wait_ge(out_ready, p + 1)
                for c in range(CHUNKS):
                    mm = pe.transpose(side[:, c * P:(c + 1) * P], heads_out[:, par, c, :], ident[:])
                mm.then_inc(side_ready, 1)

            def project_out(p):
                bank_free(p, "op")
                for c in range(CHUNKS):
                    tok = slice(c * P, (c + 1) * P)
                    mm = three_products(pe, side[:, tok], ot_hi[:, tok], ot_lo[:, tok], w["o_hi"][:], w["o_lo"][:])
                mm.then_inc(side_ready, 1)

            def score(b, par, u):
                c, half = u // 2, u % 2
                if u == 0:
                    pe.wait_ge(stack_ready, 8 * b + 8)
                    pe.wait_ge(k_heads_ready, 4 * b + 4)
                at_least(pe, exp_ready, UH * (UNITS * b + u - 1))
                for j in range(2):
                    g = 2 * half + j
                    mm = pe.matmul(scores[:, u % 2, 4 * j:4 * j + 4, :], q_stack[:, par, g, c * P:(c + 1) * P],
                                   k_heads[:, par, g, :, c * P:(c + 1) * P], start=True, stop=True)
                mm.then_inc(scores_ready, 1)

            def turn(b, u):
                at_least(pe, pt_split, UNITS * b + u)
                for h in range(UH):
                    pe.wait_ge(exp_ready, UH * (UNITS * b + u) + h + 1)
                    mm = pe.transpose(pt[:, h, :], probs[:, u % 2, h, :], ident[:])
                mm.then_inc(pt_ready, 1)

            def values(b, par, u):
                c, half = u // 2, u % 2
                if u == 0:
                    pe.wait_ge(v_split, b + 1)
                pe.wait_ge(pt_split, UNITS * b + u + 1)
                at_least(pe, intra_ready, UNITS * b + u)
                for h in range(UH):
                    hh = UH * half + h
                    p_hi, p_lo = pt_hi[:, u % 2, h, :], pt_lo[:, u % 2, h, :]
                    pe.matmul(pv[:, h, 0:VC], p_hi, v_hi[:, par, c, hh, :], start=True, stop=False)
                    pe.matmul(pv[:, h, 0:B_HEAD], p_hi, v_lo[:, par, c, hh, :], start=False, stop=False)
                    mm = pe.matmul(pv[:, h, 0:VC], p_lo, v_hi[:, par, c, hh, :], start=False, stop=True)
                mm.then_inc(pv_ready, 1)

            def step(b, par):
                nxt = 1 - par
                none = lambda: None
                first_of = (lambda: turn_x(b + 1), lambda: project("k", 1, b + 1), lambda: project("k", 3, b + 1),
                            lambda: project("q", 1, b + 1), lambda: project("q", 3, b + 1),
                            none, none, none)
                second_of = (lambda: project("k", 0, b + 1), lambda: project("k", 2, b + 1),
                             lambda: project("q", 0, b + 1), lambda: project("q", 2, b + 1),
                             lambda: project_v(b + 1), lambda: inter_scores(b + 1, nxt), none,
                             lambda: value_means(b + 1, nxt))
                for u in range(UNITS):
                    turn(b, u)
                    if not is_last(b):
                        first_of[u]()
                    if u == 5:
                        turn_inter(b)
                    if u == 6:
                        inter_product(b)
                    if u == 7 and not is_first(b):
                        project_out(b - 1)
                    b2, u2 = unit_after(b, u, 2)
                    if not (is_last(b) and u >= UNITS - 2):
                        score(b2, par if u < UNITS - 2 else nxt, u2)
                    if not is_last(b):
                        second_of[u]()
                    if u == 6 and not is_first(b):
                        turn_out(b - 1, nxt)
                    if u == 1 and is_first(b):
                        pe.wait_ge(means_taken, 2)
                    if u == 4 and not is_last(b):
                        key_means(b + 1)
                    if u > 0:
                        values(b, par, u - 1)
                    elif not is_first(b):
                        values(b - 1, nxt, UNITS - 1)

            def ahead():
                turn_x(0)
                for name in ("k", "q"):
                    for g in range(B_GROUPS):
                        project(name, g, 0)
                key_means(0)
                project_v(0)
                inter_scores(0, 0)
                value_means(0, 0)
                score(0, 0, 0)
                score(0, 0, 1)

            def tail():
                values(SEQS - 1, 1, UNITS - 1)
                turn_out(SEQS - 1, 1)
                project_out(SEQS - 1)

            run(pe, ahead, step, tail)

        @block.scalar
        def _(act):
            def x_hi(n):
                act.wait_ge(side_ready, all_of(n, "xt") + 1)
                act.activation(xt_hi[:], side[:], ACT.Copy).then_inc(norm.hi_ready, 1)

            def biased(name, g, n):
                i = g + (0 if name == "k" else B_GROUPS)
                act.wait_ge(side_ready, all_of(n, f"{name}{g}") + 1)
                at_least(act, stack_ready, 8 * n + i - 3)
                act.activation(full[:, g, :], side[:], ACT.Identity, bias=w[f"bias_{name}"][:, g:g + 1],
                               scale=(1.0 if name == "k" else B_SCALE) / WSCALE).then_inc(act_took, 1)

            def inter_exps(n):
                act.wait_ge(inter_steps, 5 * n + 2)
                act.activation(inter_exp[:], inter[:], ACT.Exp).then_inc(inter_exp_ready, 1)

            def inter_hi(n):
                act.wait_ge(side_ready, all_of(n, "at") + 1)
                act.activation(at_hi[:], side[0:INTER, :], ACT.Copy).then_inc(at_hi_ready, 1)

            def inter_copy(n, par):
                act.wait_ge(side_ready, all_of(n, "io") + 1)
                act.activation(inter_out[:, par, :, :].rearrange("p c f -> p (c f)"), side[:],
                               ACT.Copy).then_inc(act_took, 1)

            def out_hi(p):
                act.wait_ge(side_ready, all_of(p, "ot") + 1)
                act.activation(ot_hi[:], side[:], ACT.Copy).then_inc(ot_hi_ready, 1)

            def value_hi(n, par):
                act.wait_ge(dve_took, uses(n, "v")[1] + 1)
                at_least(act, pv_ready, UNITS * (n - 1))
                act.activation(v_hi[:, par, :, :, 0:B_HEAD],
                               v_full[:].rearrange("p c (h e) -> p c h e", h=B_HEADS),
                               ACT.Copy).then_inc(v_hi_ready, 1)

            def exps(b, u):
                act.wait_ge(max_ready, UNITS * b + u + 1)
                at_least(act, pt_ready, UNITS * b + u - 1)
                for h in range(UH):
                    act.activation(probs[:, u % 2, h, :], scores[:, u % 2, h, :], ACT.Exp,
                                   bias=neg_max[:, u % 2, h:h + 1]).then_inc(exp_ready, 1)

            def probs_hi(b, u):
                act.wait_ge(pt_ready, UNITS * b + u + 1)
                at_least(act, pv_ready, UNITS * b + u - 1)
                act.activation(pt_hi[:, u % 2, :, :], pt[:], ACT.Copy).then_inc(pt_hi_ready, 1)

            def step(b, par):
                nxt = 1 - par
                n = b + 1
                none = lambda: None
                early = (lambda: x_hi(n), lambda: biased("k", 1, n), lambda: biased("k", 3, n),
                         lambda: biased("q", 1, n), lambda: biased("q", 3, n), none, none, none)
                late = (lambda: biased("k", 0, n), lambda: biased("k", 2, n), lambda: biased("q", 0, n),
                        lambda: biased("q", 2, n), none, lambda: value_hi(n, nxt), none,
                        lambda: inter_exps(n))
                for u in range(UNITS):
                    probs_hi(b, u)
                    if u == 5:
                        inter_hi(b)
                    if u == 6:
                        inter_copy(b, par)
                    if not is_last(b):
                        early[u]()
                    if not (is_last(b) and u == UNITS - 1):
                        exps(*unit_after(b, u, 1))
                    if not is_last(b):
                        late[u]()
                    if u == 6 and not is_first(b):
                        out_hi(b - 1)

            def ahead():
                act.wait_ge(ones_set, 1)
                x_hi(0)
                for name in ("k", "q"):
                    for g in range(B_GROUPS):
                        biased(name, g, 0)
                value_hi(0, 0)
                inter_exps(0)
                exps(0, 0)

            run(act, ahead, step, lambda: out_hi(SEQS - 1))

        @block.gpsimd
        def _(pool):
            def add_bias(n):
                pool.wait_ge(norm.normed_ready, TPB * n + TPB)
                x4 = x_block(n)
                pool.tensor_tensor(x4, x4, w["bias_o"][:].unsqueeze(1).to_broadcast([P, TPB, DIM]),
                                   ALU.add).then_inc(bias_added, 1)

            def stack_k(g, n):
                pool.wait_ge(k_lower_ready, B_GROUPS * n + g + 1)
                at_least(pool, k_heads_ready, 4 * n)
                pool.tensor_tensor(k_stack[:, g, :], full[:, g, :], lower[:, g, :], ALU.subtract).then_inc(stack_ready, 1)

            def stack_q(g, n, par):
                pool.wait_ge(act_took, uses(n, f"q{g}")[2] + 1)
                pool.tensor_tensor(lower[:, g, :], full[:, g, :], w["lower_rows"][:, 1:2].to_broadcast([P, SEQ]),
                                   ALU.mult).then_inc(q_lower_ready, 1)
                pool.wait_ge(q_lower_ready, B_GROUPS * n + g + 1)
                at_least(pool, scores_ready, UNITS * (n - 1))
                pool.tensor_tensor(q_stack[:, par, g, :], full[:, g, :], lower[:, g, :],
                                   ALU.subtract).then_inc(stack_ready, 1)

            def add_inter(p, par):
                pool.wait_ge(intra_ready, UNITS * p + UNITS)
                pool.wait_ge(act_took, uses(p, "io")[2] + 1)
                pool.tensor_tensor(heads_out[:, par, :, :], heads_out[:, par, :, :], inter_out[:, par, :, :],
                                  ALU.add).then_inc(out_ready, 1)

            def value_lo(n, par):
                pool.wait_ge(v_hi_ready, n + 1)
                pool.tensor_tensor(v_lo[:, par, :, :, :].rearrange("p c h e -> p (c h) e"),
                                  v_full[:].rearrange("p c (h e) -> p (c h) e", h=B_HEADS),
                                  v_hi[:, par, :, :, 0:B_HEAD].rearrange("p c h e -> p (c h) e"),
                                  ALU.subtract).then_inc(v_split, 1)

            def step(b, par):
                n = b + 1
                if not is_last(b):
                    add_bias(n)
                    for g in range(B_GROUPS):
                        stack_k(g, n)
                    if not is_first(b):
                        add_inter(b - 1, 1 - par)
                    if not (isinstance(b, int) and b >= SEQS - 2):
                        norm.pool_rstd(pool, b + 2)
                    for g in range(B_GROUPS):
                        stack_q(g, n, 1 - par)
                    value_lo(n, 1 - par)

                else:
                    add_inter(b - 1, 1 - par)

            def ahead():
                norm.pool_rstd(pool, 0)
                add_bias(0)
                norm.pool_rstd(pool, 1)
                for g in range(B_GROUPS):
                    stack_k(g, 0)
                for g in range(B_GROUPS):
                    stack_q(g, 0, 0)
                value_lo(0, 0)

            run(pool, ahead, step, lambda: add_inter(SEQS - 1, 1))

        @block.vector
        def _(dve):
            def x_lo_and_sums(n):
                dve.wait_ge(norm.hi_ready, n + 1)
                dve.tensor_tensor(xt_lo[:], side[:], xt_hi[:], ALU.subtract).then_inc(norm.xt_ready, 1)
                dve.tensor_reduce(xm[:], side[:].rearrange("p (c t) -> p c t", c=CHUNKS), AX.X,
                                  ALU.add).then_inc(dve_took, 1)

            def x_means(n):
                dve.wait_ge(dve_took, uses(n, "xt")[1] + 1)
                dve.tensor_scalar(xm_hi[:], xm[:], 1.0 / CHUNK, None, ALU.mult).then_inc(xm_split, 1)
                dve.wait_ge(xm_split, 2 * n + 1)
                dve.scalar_tensor_tensor(out=xm_lo[:], in0=xm[:], scalar=1.0 / CHUNK, in1=xm_hi[:], op0=ALU.mult,
                                         op1=ALU.subtract).then_inc(xm_split, 1)

            def lower_k(g, n):
                dve.wait_ge(act_took, uses(n, f"k{g}")[2] + 1)
                dve.tensor_scalar(lower[:, g, :], full[:, g, :], w["lower_rows"][:, 0:1], None,
                                  ALU.mult).then_inc(k_lower_ready, 1)

            def heads_of_k(n, par, heads):
                dve.wait_ge(stack_ready, 8 * n + B_GROUPS)
                if not is_first(n):
                    at_least(dve, scores_ready, UNITS * (n - 1))
                for r in heads:
                    dve.tensor_scalar(k_heads[:, par, :, r, :], k_stack[:], w["head_rows"][:, r:r + 1], None,
                                      ALU.mult).then_inc(k_heads_ready, 1)

            def means_of_k(n):
                dve.wait_ge(means_ready, 2 * n + 1)
                at_least(dve, pv_ready, UNITS * (n - 1) + 4)
                flat = lambda t: t[:].rearrange("p g c -> p (g c)")
                dve.scalar_tensor_tensor(out=km_full[:], in0=k_means.rearrange(
                    "p (g c) -> p g c", g=B_GROUPS), scalar=1.0 / WSCALE,
                    in1=w["bias_k"][:].unsqueeze(2).to_broadcast([P, B_GROUPS, CHUNKS]), op0=ALU.mult,
                    op1=ALU.add).then_inc(means_taken, 1)
                dve.wait_ge(means_taken, 2 * n + 1)
                dve.tensor_scalar(flat(km_lower), flat(km_full), w["lower_rows"][:, 0:1], None,
                                  ALU.mult).then_inc(km_steps, 1)
                dve.wait_ge(km_steps, 6 * n + 1)
                dve.tensor_tensor(flat(km_stack), flat(km_full), flat(km_lower), ALU.subtract).then_inc(km_steps, 1)
                dve.wait_ge(km_steps, 6 * n + 2)
                for r in range(4):
                    dve.tensor_scalar(km_heads[:, :, r, :], km_stack[:], w["head_rows"][:, r:r + 1], None,
                                      ALU.mult).then_inc(km_steps, 1)

            def value_full(n):
                dve.wait_ge(side_ready, all_of(n, "v") + 1)
                if not is_first(n):
                    dve.wait_ge(v_split, n)
                dve.scalar_tensor_tensor(out=v_full[:], in0=side[:].rearrange("p (c f) -> p c f", c=CHUNKS),
                                         scalar=1.0 / WSCALE,
                                         in1=w["bias_v"][:].unsqueeze(1).to_broadcast([P, CHUNKS, DIM]),
                                         op0=ALU.mult, op1=ALU.add).then_inc(dve_took, 1)

            def inter_shift(n):
                dve.wait_ge(side_ready, all_of(n, "si") + 1)
                quads = lambda t: t[:].rearrange("p (i j) -> p i j", j=CHUNKS)
                if not is_first(n):
                    dve.wait_ge(inter_exp_ready, n)
                dve.tensor_tensor(inter[:], side[:, 0:CHUNKS * INTER], w["causal"][:], ALU.add).then_inc(dve_took, 1)
                dve.wait_ge(dve_took, uses(n, "si")[1] + 1)
                dve.tensor_reduce(inter_max[:], quads(inter), AX.X, ALU.max).then_inc(inter_steps, 1)
                dve.wait_ge(inter_steps, 5 * n + 1)
                dve.tensor_tensor(quads(inter), quads(inter),
                                  inter_max[:].unsqueeze(2).to_broadcast([P, INTER, CHUNKS]),
                                  ALU.subtract).then_inc(inter_steps, 1)

            def inter_normalise(n):
                quads = lambda t: t[:].rearrange("p (i j) -> p i j", j=CHUNKS)
                dve.wait_ge(inter_exp_ready, n + 1)
                dve.tensor_reduce(inter_sum[:], quads(inter_exp), AX.X, ALU.add).then_inc(inter_steps, 1)
                dve.wait_ge(inter_steps, 5 * n + 3)
                dve.reciprocal(inter_inv[:], inter_sum[:]).then_inc(inter_steps, 1)
                dve.wait_ge(inter_steps, 5 * n + 4)
                dve.tensor_tensor(inter_probs[:, 0:CHUNKS, :].rearrange("p c (i j) -> p (c i) j", j=CHUNKS), quads(inter_exp),
                                  inter_inv[:].unsqueeze(2).to_broadcast([P, INTER, CHUNKS]),
                                  ALU.mult).then_inc(inter_steps, 1)

            def means_of_v(n):
                dve.wait_ge(means_ready, 2 * n + 2)
                at_least(dve, pv_ready, UNITS * (n - 1) + 7)
                if not is_first(n):
                    dve.wait_ge(act_took, uses(n - 1, "io")[2] + 1)
                dve.tensor_tensor(vm_full[:], v_means, w["own_head"][:], ALU.mult).then_inc(means_taken, 1)
                dve.wait_ge(means_taken, 2 * n + 2)
                dve.tensor_copy(vm_hi[:], vm_full[:]).then_inc(vm_steps, 1)
                dve.wait_ge(vm_steps, 2 * n + 1)
                dve.tensor_tensor(vm_lo[:], vm_full[:], vm_hi[:], ALU.subtract).then_inc(vm_steps, 1)

            def inter_lo(n):
                dve.wait_ge(at_hi_ready, n + 1)
                dve.tensor_tensor(at_lo[:], side[0:INTER, :], at_hi[:], ALU.subtract).then_inc(dve_took, 1)

            def out_lo(p):
                dve.wait_ge(ot_hi_ready, p + 1)
                dve.tensor_tensor(ot_lo[:], side[:], ot_hi[:], ALU.subtract).then_inc(dve_took, 1)

            def add_out(p):
                dve.wait_ge(side_ready, all_of(p, "op") + 1)
                dve.wait_ge(bias_added, p + 1)
                x4 = x_block(p)
                dve.scalar_tensor_tensor(out=x4, in0=side[:].rearrange("p (t f) -> p t f", t=TPB),
                                         scalar=1.0 / WSCALE, in1=x4, op0=ALU.mult, op1=ALU.add).then_inc(dve_took, 1)

            def maxima(b, u):
                dve.wait_ge(scores_ready, UNITS * b + u + 1)
                at_least(dve, exp_ready, UH * (UNITS * b + u - 1))
                dve.tensor_reduce(neg_max[:, u % 2, :], scores[:, u % 2, :, :], AX.X, ALU.max,
                                  negate=True).then_inc(max_ready, 1)

            def probs_lo(b, u):
                dve.wait_ge(pt_hi_ready, UNITS * b + u + 1)
                dve.tensor_tensor(pt_lo[:, u % 2, :, :], pt[:], pt_hi[:, u % 2, :, :],
                                  ALU.subtract).then_inc(pt_split, 1)

            def normalise(b, par, u):
                c, half = u // 2, u % 2
                dve.wait_ge(pv_ready, UNITS * b + u + 1)
                dve.reciprocal(inv_sum[:], pv[:, :, B_HEAD]).then_inc(inv_ready, 1)
                dve.wait_ge(inv_ready, UNITS * b + u + 1)
                cols = slice(half * UH * B_HEAD, (half + 1) * UH * B_HEAD)
                dve.tensor_tensor(heads_out[:, par, c, cols].rearrange("p (h e) -> p h e", h=UH), pv[:, :, 0:B_HEAD],
                                  inv_sum[:].unsqueeze(2).to_broadcast([P, UH, B_HEAD]),
                                  ALU.mult).then_inc(intra_ready, 1)

            def step(b, par):
                nxt, n = 1 - par, b + 1
                none = lambda: None
                early = (none, lambda: lower_k(0, n), lambda: lower_k(2, n), none, none, none, none, none)
                late = (none, lambda: lower_k(1, n), lambda: lower_k(3, n), lambda: heads_of_k(n, nxt, (0, 1, 2)),
                        lambda: means_of_k(n),
                        lambda: (heads_of_k(n, nxt, (3,)), inter_shift(n)), none, lambda: means_of_v(n))
                for u in range(UNITS):
                    if u == 7 and not is_first(b):
                        out_lo(b - 1)
                    if u == 0 and not is_last(b):
                        x_lo_and_sums(n)
                    if u == 5 and not is_last(b):
                        value_full(n)
                    probs_lo(b, u)
                    if u == 5:
                        inter_lo(b)
                    if u == 0 and not is_last(b):
                        x_means(n)
                    if not is_last(b):
                        early[u]()
                    b2, u2 = unit_after(b, u, 2)
                    if not (is_last(b) and u >= UNITS - 2):
                        maxima(b2, u2)
                    if u == 7 and not is_first(b):
                        add_out(b - 1)
                    if not is_last(b):
                        late[u]()
                    if u > 0:
                        normalise(b, par, u - 1)
                    elif not is_first(b):
                        normalise(b - 1, nxt, UNITS - 1)
                    if u == 0:
                        inter_normalise(b)
                    if not (isinstance(b, int) and b >= SEQS - 2):
                        if u == 1:
                            norm.dve_moments(dve, b + 2, x_block(b + 2))
                        if u == 6:
                            norm.dve_apply(dve, b + 2, x_block(b + 2))

            def ahead():
                dve.memset(v_hi[:], 1.0).then_inc(ones_set, 1)
                dve.memset(inter_probs[:, CHUNKS, :], 0.0).then_inc(ones_set, 1)
                norm.dve_moments(dve, 0, x_block(0))
                norm.dve_apply(dve, 0, x_block(0))
                x_lo_and_sums(0)
                x_means(0)
                norm.dve_moments(dve, 1, x_block(1))
                for g in range(B_GROUPS):
                    lower_k(g, 0)
                norm.dve_apply(dve, 1, x_block(1))
                heads_of_k(0, 0, range(4))
                means_of_k(0)
                value_full(0)
                inter_shift(0)
                means_of_v(0)
                maxima(0, 0)
                maxima(0, 1)

            def tail():
                normalise(SEQS - 1, 1, UNITS - 1)
                out_lo(SEQS - 1)
                add_out(SEQS - 1)

            run(dve, ahead, step, tail)


def program(nc, d, out):
    with ExitStack() as ctx:
        s = Space(nc, ctx, "m")
        x_all = s.sb("x_all", [P, TILES, DIM], F32)
        ident = s.sb("ident", [P, P], F32)
        minus_half = s.sb("minus_half", [P, TPB], F32)
        INTER = B_HEADS * CHUNKS
        wf = {"sign1": s.sb("sign1", [P, HIDDEN], F16), "sign2": s.sb("sign2", [P, HT, DIM], F16),
              "alpha1": s.sb("alpha1", [P, HT], F32), "alpha2": s.sb("alpha2", [P, DIM], F32),
              "b1": s.sb("b1", [P, HT], F32), "b2": s.sb("b2", [P, DIM], F32)}
        wb = {"k_hi": s.sb("k_hi", [P, HIDDEN], F16), "k_lo": s.sb("k_lo", [P, HIDDEN], F16),
              "q_hi": s.sb("q_hi", [P, HIDDEN], F16), "q_lo": s.sb("q_lo", [P, HIDDEN], F16),
              "v_hi": s.sb("v_hi", [P, DIM], F16), "v_lo": s.sb("v_lo", [P, DIM], F16),
              "o_hi": s.sb("o_hi", [P, DIM], F16), "o_lo": s.sb("o_lo", [P, DIM], F16),
              "bias_k": s.sb("bias_k", [P, B_GROUPS], F32), "bias_q": s.sb("bias_q", [P, B_GROUPS], F32),
              "bias_v": s.sb("bias_v", [P, DIM], F32), "bias_o": s.sb("bias_o", [P, DIM], F32),
              "lower_rows": s.sb("lower_rows", [P, 2], F32), "head_rows": s.sb("head_rows", [P, 4], F32),
              "mean_select": s.sb("mean_select", [P, CHUNKS, INTER], F16),
              "causal": s.sb("causal", [P, CHUNKS * INTER], F32),
              "own_head": s.sb("own_head", [INTER, DIM], F32)}
        with ExitStack() as keep:
            a = Space(nc, keep, "aw")
            wa = {"xt_hi": a.sb("xt_hi", [P, TOKENS], F16), "xt_lo": a.sb("xt_lo", [P, TOKENS], F16),
                  "w_hi": a.sb("w_hi", [P, 5, A_INNER], F16), "w_lo": a.sb("w_lo", [P, 5, A_INNER], F16),
                  "wo_hi": a.sb("wo_hi", [P, A_PAIRS, DIM], F16), "wo_lo": a.sb("wo_lo", [P, A_PAIRS, DIM], F16),
                  "cos": a.sb("cos", [P, 2, SEQ], F32), "sin": a.sb("sin", [P, 2, SEQ], F32),
                  "four": a.sb("four", [P, 2, SEQ], F32)}
            prepare(nc, d, x_all, ident, minus_half, wa, wf, wb)
            attention_a(nc, x_all, ident, wa)
        feed_forward(nc, x_all, ident, minus_half, wf, "f1")
        attention_b(nc, x_all, ident, minus_half, wb)
        feed_forward(nc, x_all, ident, minus_half, wf, "f2", out)


def layouts(a):
    f = {k[3:]: np.ascontiguousarray(v) for k, v in a.items()}
    d = {}
    d["x"] = f["attn_a_x"].reshape(TILES, P, DIM).transpose(1, 0, 2)
    wq, wk, wv = f["attn_a_w_qkv"].reshape(3, A_HEADS, A_HEAD, DIM)
    order = np.concatenate([np.arange(1, A_HEAD, 2), np.arange(0, A_HEAD, 2)])
    kinds = [wq, wq[:, order], wk, wk[:, order], wv]
    d["w_a"] = np.stack([w.reshape(A_INNER, DIM).T for w in kinds], axis=1)
    d["wo_a"] = f["attn_a_w_out"].T.reshape(A_PAIRS, P, DIM).transpose(1, 0, 2)
    d["b_out_a"] = np.broadcast_to(f["attn_a_b_out"], (P, DIM))
    d["w_four"] = np.tile(f["attn_a_w_fproj"].T, (1, 2))
    d["b_four"] = np.tile(f["attn_a_b_fproj"], 2)[:, None]
    pos = np.arange(SEQ, dtype=np.float32)[:, None]
    freqs = np.float32(10000.0) ** (-np.arange(0, A_HEAD, 2, dtype=np.float32) / np.float32(A_HEAD))
    angles = pos * freqs
    sign = np.where(np.arange(A_HEAD) < A_HEAD // 2, -1.0, 1.0)[:, None]
    cos = np.repeat(np.cos(angles), 2, axis=1).T
    sin = np.repeat(np.sin(angles), 2, axis=1).T * sign
    scales = np.array([A_SCALE, 1.0])[:, None, None] / WSCALE
    d["cos"] = (np.tile(cos, (2, 1))[None] * scales).astype(np.float32)
    d["sin"] = (np.tile(sin, (2, 1))[None] * scales).astype(np.float32)
    harmonics = pos * np.arange(1, FREQS + 1, dtype=np.float32)
    d["fourier"] = np.concatenate([np.sin(harmonics), np.cos(harmonics)], axis=-1).T
    d["ident"] = np.eye(P, dtype=np.float32)
    w1, w2 = f["ffn_w1"], f["ffn_w2"]
    d["w1"] = w1.reshape(HT, P, DIM).transpose(1, 0, 2)
    d["w1t"] = w1.T
    d["w2t"] = w2.T.reshape(HT, P, DIM).transpose(1, 0, 2)
    d["b1"] = f["ffn_b1"].reshape(HT, P).T
    d["b2"] = np.broadcast_to(f["ffn_b2"], (P, DIM))

    def stacked(t):
        t = t.reshape(B_GROUPS, 4, 1, B_HEAD, -1)
        return np.concatenate([t, t, t, np.zeros_like(t)], axis=2).reshape(HIDDEN, -1)

    for name in "qk":
        d[f"w{name}_b"] = stacked(f[f"attn_b_w{name}"]).T
        d[f"bias_{name}"] = stacked(f[f"attn_b_b{name}"]).reshape(B_GROUPS, P).T
    for name in "vo":
        d[f"w{name}_b"] = f[f"attn_b_w{name}"].T
        d[f"bias_{name}"] = np.broadcast_to(f[f"attn_b_b{name}"], (P, DIM))
    row = np.arange(P)
    copy = row % 32 // B_HEAD
    d["lower_rows"] = np.stack([copy == 1, copy == 2], axis=1).astype(np.float32)
    d["head_rows"] = (row[:, None] // 32 == np.arange(4)).astype(np.float32)
    own, chunk = np.divmod(np.arange(B_HEADS * CHUNKS), CHUNKS)
    c = np.arange(CHUNKS)
    d["mean_select"] = np.broadcast_to((chunk == c[:, None]) / CHUNK, (P, CHUNKS, B_HEADS * CHUNKS)).astype(np.float16)
    d["causal"] = np.broadcast_to(np.where(chunk > c[:, None], -1e30, 0.0).reshape(-1), (P, CHUNKS * B_HEADS * CHUNKS))
    d["causal"] = d["causal"].astype(np.float32)
    d["own_head"] = (own[:, None] == np.arange(DIM) // B_HEAD).astype(np.float32)
    return {k: np.ascontiguousarray(v) for k, v in d.items()}


def kernel(**inputs):
    import concourse.bacc as bacc
    from concourse.bass_utils import run_bass_kernel_spmd

    nc = bacc.Bacc("TRN2", target_bir_lowering=False, num_devices=1)
    arrays = {f"in_{k}": v for k, v in layouts(inputs).items()}
    d = {k[3:]: nc.dram_tensor(k, v.shape, mybir.dt.from_np(v.dtype), kind="ExternalInput").ap()
         for k, v in arrays.items()}
    out = nc.dram_tensor("out_x", (P, TILES, DIM), F32, kind="ExternalOutput").ap()
    program(nc, d, out)
    r = run_bass_kernel_spmd(nc, [arrays], core_ids=[0])
    got = r.results[0]["out_x"]
    return np.ascontiguousarray(got.transpose(1, 0, 2)).reshape(BATCH, SEQ, DIM)
```
